# Optimizing a Trainium2 kernel written in Bass

```python
import numpy as np
import jax
import jax.numpy as jnp

def _softmax(x, axis=-1):
    return jax.nn.softmax(x, axis=axis)

def _gelu(x):
    return jax.nn.gelu(x, approximate=True)

def _silu(x):
    return jax.nn.silu(x)

def _sigmoid(x):
    return jax.nn.sigmoid(x)

def _layernorm(x, axis=-1, eps=1e-05):
    m = jnp.mean(x, axis=axis, keepdims=True)
    v = jnp.var(x, axis=axis, keepdims=True)
    return (x - m) / jnp.sqrt(v + eps)

def _scatter_add(tgt, idx, src, axis=0):
    return tgt.at[idx].add(src)

def _segment_sum(src, seg, n):
    return jax.ops.segment_sum(src, seg, n)
kernel_name = 'mk_gps_d1_gnn_r64_24c732'

def setup_inputs(seed: int=0):
    np.random.seed(seed)
    _w = jnp.asarray

    def _rec_inputs():
        import jax
        import jax.numpy as jnp
        _gk = jax.random.key(seed)
        x = -0.0003019 + 1 * jax.random.normal(jax.random.fold_in(_gk, 1), (10000, 1024), jnp.float32)
        src = jax.random.randint(jax.random.fold_in(_gk, 2), (2500,), 0, 10000, jnp.int32)
        dst = jnp.minimum((10000 * jax.random.uniform(jax.random.fold_in(_gk, 3), (2500,)) ** 2.0).astype(jnp.int32), 9999)
        _o = jnp.argsort(dst, stable=True)
        src = src[_o]
        dst = dst[_o]
        return (x, src, dst)
    x, src, dst = _rec_inputs()

    def _L0_gnn_setup():
        import jax, jax.numpy as jnp
        import numpy as np
        N = 20000
        E = 5000
        D_IN = 1024
        D_OUT = 1024
        key = jax.random.key(seed)
        k1, k2, k3, k4 = jax.random.split(key, 4)
        x = jax.random.normal(k1, (N, D_IN), dtype=jnp.float32)
        edge_index = jax.random.randint(k2, (2, E), 0, N, dtype=jnp.int64)
        W = jax.random.normal(k3, (D_OUT, D_IN), dtype=jnp.float32) * (1.0 / np.sqrt(D_IN))
        b = jax.random.normal(k4, (D_OUT,), dtype=jnp.float32) * 0.01
        return {'x': x, 'edge_index': edge_index, 'W': W, 'b': b}
    _L0_gnn_all = _L0_gnn_setup()
    _L0_gnn_in = {k: v for k, v in _L0_gnn_all.items() if k in ('W', 'b')}
    del _L0_gnn_all

    def _L0_mix_setup():
        import jax, jax.numpy as jnp
        import numpy as np
        NUM_HEADS = 16
        KEY_DIM = 64
        EPS = 1e-06
        key = jax.random.key(seed)
        k0, k1, k2, k3, k4 = jax.random.split(key, 5)
        B, S, E = (4, 64, NUM_HEADS * KEY_DIM)
        scale = 1.0 / np.sqrt(KEY_DIM)
        return {'query': jax.random.normal(k0, (B, S, E), dtype=jnp.float32), 'Wq': jax.random.normal(k1, (NUM_HEADS, KEY_DIM, KEY_DIM), dtype=jnp.float32) * scale, 'Wk': jax.random.normal(k2, (NUM_HEADS, KEY_DIM, KEY_DIM), dtype=jnp.float32) * scale, 'Wv': jax.random.normal(k3, (NUM_HEADS, KEY_DIM, KEY_DIM), dtype=jnp.float32) * scale, 'Wo': jax.random.normal(k4, (E, E), dtype=jnp.float32) * (1.0 / np.sqrt(E))}
    _L0_mix_all = _L0_mix_setup()
    _L0_mix_in = {k: v for k, v in _L0_mix_all.items() if k in ('Wq', 'Wk', 'Wv', 'Wo')}
    del _L0_mix_all

    def _L0_ffn_setup():
        import jax, jax.numpy as jnp
        import numpy as np
        MODEL_DIM = 1024
        HIDDEN = 32
        NUM_GROUPS = 2
        EXPERTS_PER_GP = 4
        NUM_EXPERTS = NUM_GROUPS * EXPERTS_PER_GP
        TOP_K = 2
        B, T = (2, 32)

        def _swiglu(x):
            a, b = jnp.split(x, 2, axis=-1)
            return jax.nn.silu(a) * b
        key = jax.random.key(seed)
        ks = jax.random.split(key, 7)
        s = 0.02
        return {'x': jax.random.normal(ks[0], (B, T, MODEL_DIM), jnp.float32), 'w_in': jax.random.normal(ks[1], (HIDDEN * 2, MODEL_DIM), jnp.float32) * s, 'w_out': jax.random.normal(ks[2], (MODEL_DIM, HIDDEN), jnp.float32) * s, 'w1': jax.random.normal(ks[3], (HIDDEN * 2, MODEL_DIM), jnp.float32) * s, 'w2': jax.random.normal(ks[4], (NUM_EXPERTS, MODEL_DIM, HIDDEN), jnp.float32) * s, 'wg': jax.random.normal(ks[5], (NUM_GROUPS, MODEL_DIM), jnp.float32) * s, 'we': jax.random.normal(ks[6], (NUM_EXPERTS, MODEL_DIM), jnp.float32) * s, 'gb': jnp.zeros((NUM_GROUPS,), jnp.float32), 'eb': jnp.zeros((NUM_EXPERTS,), jnp.float32)}
    _L0_ffn_all = _L0_ffn_setup()
    _L0_ffn_in = {k: v for k, v in _L0_ffn_all.items() if k in ('w_in', 'w_out', 'w1', 'w2', 'wg', 'we', 'gb', 'eb')}
    del _L0_ffn_all
    return {'x': x, 'src': src, 'dst': dst, 'L0_gnn_W': _L0_gnn_in['W'], 'L0_gnn_b': _L0_gnn_in['b'], 'L0_mix_Wq': _L0_mix_in['Wq'], 'L0_mix_Wk': _L0_mix_in['Wk'], 'L0_mix_Wv': _L0_mix_in['Wv'], 'L0_mix_Wo': _L0_mix_in['Wo'], 'L0_ffn_w_in': _L0_ffn_in['w_in'], 'L0_ffn_w_out': _L0_ffn_in['w_out'], 'L0_ffn_w1': _L0_ffn_in['w1'], 'L0_ffn_w2': _L0_ffn_in['w2'], 'L0_ffn_wg': _L0_ffn_in['wg'], 'L0_ffn_we': _L0_ffn_in['we'], 'L0_ffn_gb': _L0_ffn_in['gb'], 'L0_ffn_eb': _L0_ffn_in['eb']}

def reference(x, src, dst, L0_gnn_W, L0_gnn_b, L0_mix_Wq, L0_mix_Wk, L0_mix_Wv, L0_mix_Wo, L0_ffn_w_in, L0_ffn_w_out, L0_ffn_w1, L0_ffn_w2, L0_ffn_wg, L0_ffn_we, L0_ffn_gb, L0_ffn_eb):
    import jax
    import jax.numpy as jnp

    def _L0_gnn_ref(x, edge_index, W, b):
        import jax, jax.numpy as jnp
        import numpy as np
        N = 20000
        E = 5000
        D_IN = 1024
        D_OUT = 1024
        num_nodes = x.shape[0]
        self_idx = jnp.arange(num_nodes, dtype=edge_index.dtype)
        ei = jnp.concatenate([edge_index, jnp.stack([self_idx, self_idx], axis=0)], axis=1)
        row, col = (ei[0], ei[1])
        h = jnp.einsum('nd,od->no', x, W) + b
        deg = jnp.zeros((num_nodes,), dtype=h.dtype).at[row].add(1.0)
        deg_inv_sqrt = deg ** (-0.5)
        norm = deg_inv_sqrt[row] * deg_inv_sqrt[col]
        msg = norm[:, None] * h[col]
        out = jax.ops.segment_sum(msg, row, num_segments=num_nodes)
        return out

    def _L0_mix_ref(query, Wq, Wk, Wv, Wo):
        import jax, jax.numpy as jnp
        import numpy as np
        NUM_HEADS = 16
        KEY_DIM = 64
        EPS = 1e-06
        B, S, E = query.shape
        H, D = (NUM_HEADS, KEY_DIM)
        x = jnp.transpose(query.reshape(B, S, H, D), (0, 2, 1, 3))
        q = jnp.einsum('bhsd,hde->bhse', x, Wq)
        k = jnp.einsum('bhsd,hde->bhse', x, Wk)
        v = jnp.einsum('bhsd,hde->bhse', x, Wv)
        phi_q = jax.nn.elu(q) + 1.0
        phi_k = jax.nn.elu(k) + 1.0
        kv = jnp.einsum('bhsd,bhse->bhde', phi_k, v)
        k_sum = jnp.sum(phi_k, axis=2)
        z = jnp.einsum('bhsd,bhd->bhs', phi_q, k_sum)
        ctx = jnp.einsum('bhsd,bhde->bhse', phi_q, kv) / (z[..., None] + EPS)
        combined = jnp.transpose(ctx, (0, 2, 1, 3)).reshape(B, S, H * D)
        return combined @ Wo

    def _L0_ffn_ref(x, w_in, w_out, w1, w2, wg, we, gb, eb):
        import jax, jax.numpy as jnp
        import numpy as np
        MODEL_DIM = 1024
        HIDDEN = 32
        NUM_GROUPS = 2
        EXPERTS_PER_GP = 4
        NUM_EXPERTS = NUM_GROUPS * EXPERTS_PER_GP
        TOP_K = 2
        B, T = (2, 32)

        def _swiglu(x):
            a, b = jnp.split(x, 2, axis=-1)
            return jax.nn.silu(a) * b
        Bs, Ts, C = x.shape
        S = Bs * Ts
        flat = x.reshape(S, C)
        shared = _swiglu(flat @ w_in.T) @ w_out.T
        g_probs = jax.nn.softmax(flat @ wg.T + gb, axis=-1)
        g_idx = jnp.argmax(g_probs, axis=-1)
        e_logits = flat @ we.T + eb
        egid = jnp.arange(NUM_EXPERTS) // EXPERTS_PER_GP
        masked = jnp.where(g_idx[:, None] == egid[None, :], e_logits, -jnp.inf)
        e_probs = jax.nn.softmax(masked, axis=-1)
        g_prob = jnp.take_along_axis(g_probs, g_idx[:, None], axis=1)
        p_expert = e_probs * g_prob
        topv, topi = jax.lax.top_k(p_expert, TOP_K)
        w_se = jnp.zeros((S, NUM_EXPERTS), x.dtype).at[jnp.arange(S)[:, None], topi].add(topv)
        h = _swiglu(flat @ w1.T)
        routed = jnp.zeros_like(shared)
        for e in range(NUM_EXPERTS):
            routed = routed + h * w_se[:, e:e + 1] @ w2[e].T
        return (shared + routed).reshape(Bs, Ts, C)
    edge_index = jnp.stack([src, dst])
    xn = _layernorm(x, axis=-1)
    x = x + _L0_gnn_ref(xn, edge_index, L0_gnn_W, L0_gnn_b) + _L0_mix_ref(xn[None], L0_mix_Wq, L0_mix_Wk, L0_mix_Wv, L0_mix_Wo)[0]
    x = x + _L0_ffn_ref(_layernorm(x, axis=-1)[None], L0_ffn_w_in, L0_ffn_w_out, L0_ffn_w1, L0_ffn_w2, L0_ffn_wg, L0_ffn_we, L0_ffn_gb, L0_ffn_eb)[0]
    return x

_drawn_inputs = setup_inputs


def setup_inputs(seed=0):
    import zlib

    import numpy as np

    out = dict(_drawn_inputs(seed))
    spreads = {'L0_ffn_gb': (0.0, 0.8), 'L0_ffn_eb': (0.0, 0.8)}
    factors = {'L0_gnn_b': 7.959,
     'L0_mix_Wq': 8.0,
     'L0_mix_Wk': 6.333,
     'L0_mix_Wv': 5.086,
     'L0_mix_Wo': 4.925,
     'L0_ffn_w_in': 2.884,
     'L0_ffn_w_out': 2.754,
     'L0_ffn_w1': 8.0,
     'L0_ffn_w2': 8.0,
     'L0_ffn_wg': 8.0,
     'L0_ffn_we': 8.0}
    for name, (base, spread) in spreads.items():
        noise = np.random.default_rng([zlib.crc32(name.encode()), seed]).standard_normal(out[name].shape)
        drawn = base * np.exp(spread * noise) if base else spread * noise
        out[name] = jnp.asarray(drawn.astype(out[name].dtype))
    for name, factor in factors.items():
        out[name] = (out[name] * factor).astype(out[name].dtype)
    return out
```

```python
from contextlib import ExitStack

import concourse.bass as bass
from concourse import mybir

ALU = mybir.AluOpType
ACT = mybir.ActivationFunctionType
AX_X = mybir.AxisListType.X
F32 = mybir.dt.float32
F32R = mybir.dt.float32r
F16 = mybir.dt.float16
I32 = mybir.dt.int32
U32 = mybir.dt.uint32

P = 128
RING = 3
HALF = 512
LN_EPS = 1e-5
Z_EPS = 1e-6
Y_SCALE_MAX = 32.0
A_SCALE_MAX = float(2 ** 14)
W_TOP = float(2 ** 15)
BIG = 1e30


class Tile:

    def __init__(self, base, i=None):
        self.base, self.i = base, i
        self.slot = base % RING
        self.n = base if i is None else i * RING + base
        self.turn = base // RING if i is None else i + base // RING

    def __add__(self, d):
        return Tile(self.base + d, self.i)

    def __sub__(self, d):
        return Tile(self.base - d, self.i)

    def within(self, count):
        return self.i is not None or 0 <= self.base < count


def count_of(tile, per, k):
    return tile.n * per + k


def carry(eng, cell):
    return eng.tensor_tensor(cell[0:1, 1:2], cell[0:1, 0:1], cell[0:1, 0:1], ALU.add)


def wait(eng, sem, value):
    if not isinstance(value, int) or value > 0:
        eng.wait_ge(sem, value)


def gps_layer(nc, x, src, dst, gnn_W, gnn_b, Wq, Wk, Wv, Wo, w_in, w_out, w1, w2, wg, we, gb, eb, out):
    N, D = x.shape
    E = src.shape[0]
    H, DH = Wq.shape[0], Wq.shape[1]
    HID = w_out.shape[1]
    NEXP = w2.shape[0]
    NGRP = wg.shape[0]
    EPG = NEXP // NGRP
    C = D // P
    CH = C // 2
    NTF, REM = N // P, N % P
    NT = NTF + 1
    EP = 125
    ET = E // EP
    FIN = 4 * HID + NGRP + NEXP
    assert D == 1024 and DH == 64 and H * DH == D and REM and E == EP * ET and EPG * NGRP == NEXP
    assert NGRP == 2 and HID == 32 and NEXP == 8
    G_ROWS = (NT + 1) * P
    PAD_SRC = N

    P1_FIRST = 4
    P1_A = (NT - P1_FIRST - RING * ET - 4) // RING
    assert P1_A >= 1
    P2_FIRST = 2
    P2_TURNS = (NTF - 2 - P2_FIRST) // RING

    agg = nc.dram_tensor("agg_rows", (G_ROWS, D), F32, kind="Internal").ap()
    dis_rows = nc.dram_tensor("deg_inv_sqrt", (NT, P), F32, kind="Internal").ap()
    P1_BEFORE = P1_FIRST + RING * P1_A
    ZSTEP = min(4, (NT + 1) // P1_BEFORE)
    ZPREP = NT + 1 - ZSTEP * P1_BEFORE
    ZPARTS = 1 + P1_BEFORE

    with ExitStack() as ctx:
        def sb(name, shape, dt=F32):
            return ctx.enter_context(nc.sbuf_tensor(name, shape, dt))

        def sem(name):
            return ctx.enter_context(nc.semaphore(name))

        fT_hi = sb("fT_hi", [P, C, P], F32R)
        fT_lo = sb("fT_lo", [P, C, P], F32R)
        wq_hi = sb("wq_hi", [P, C, P], F32R)
        wq_lo = sb("wq_lo", [P, C, P], F32R)
        fin_hi = sb("fin_hi", [P, C, FIN], F32R)
        fin_lo = sb("fin_lo", [P, C, FIN], F32R)
        w2_hi = sb("w2_hi", [P, NGRP, D], F32R)
        w2_lo = sb("w2_lo", [P, NGRP, D], F32R)
        wo3 = sb("wo3", [3 * HID, D], F32R)
        hwT_hi = sb("hwT_hi", [P, NGRP, P], F32R)
        hwT_lo = sb("hwT_lo", [P, NGRP, P], F32R)
        sh3T = sb("sh3T", [3 * HID, P], F32R)
        w_hi = sb("w_hi", [P, C, D], F16)
        w_lo = sb("w_lo", [P, C, D], F16)
        mreg = sb("mreg", [P, C * D])
        m_hi = mreg[:, 0:C * D // 2].bitcast(F16).rearrange("p (c n) -> p c n", c=C)
        m_lo = mreg[:, C * D // 2:].bitcast(F16).rearrange("p (c n) -> p c n", c=C)
        XNW = C * (P + 1)
        phi1 = [mreg[:, s * D:(s + 1) * D] for s in range(RING)]
        xn1 = [mreg[:, 3 * D + s * XNW:3 * D + (s + 1) * XNW].rearrange("p (c f) -> p c f", c=C)
               for s in range(RING)]
        ex1 = mreg[:, 3 * D + 3 * XNW:4 * D + 3 * XNW]
        ohb = mreg[:, 0:ET * P].rearrange("p (t b) -> p t b", b=P)
        oha = mreg[:, ET * P:ET * (P + NT)].rearrange("p (t b) -> p t b", b=NT)
        ohn = mreg[:, ET * (P + NT):ET * (P + 2 * NT)].rearrange("p (t b) -> p t b", b=NT)
        w2rows = mreg[:, 5 * D + 768:7 * D + 768].rearrange("p (n e h) -> p n e h", n=C, e=NEXP)
        assert ET * (P + 2 * NT) <= 5 * D + 768
        zreg = sb("zreg", [P, 9 * D])
        wrows = zreg[:, 0:8 * D].rearrange("p (o i) -> p o i", o=C)
        worows = wrows
        zeros = zreg[:, 8 * D:9 * D]
        parts = zreg[:, 0:6 * D].bitcast(F16).rearrange("p (s k c n) -> p s k c n", s=RING, k=4, c=C)
        yT_hi, yT_lo, aT_hi, aT_lo = [[parts[:, s, k] for s in range(RING)] for k in range(4)]
        xp = [zreg[:, (6 + s) * D:(7 + s) * D] for s in range(RING)]
        xin = [sb(f"xin{s}", [P, D]) for s in range(RING)]
        greg = sb("greg", [P, 3 * D])
        gin = [greg[:, s * D:(s + 1) * D] for s in range(RING)]
        srcb = greg[:, 0:P * ET].bitcast(I32).rearrange("p (e t) -> p e t", t=ET)
        dgm = gin[2].rearrange("p (c n) -> p c n", c=C)
        xn = sb("xn", [P, D])
        xe = xn
        wcat1 = xn
        xn2 = sb("xn2", [P, D])
        msum = xn2
        wcat2 = xn2[0:NGRP + NEXP, :]
        phi = sb("phi", [P, D])
        x1T = phi[:, :].rearrange("p (c n) -> p c n", c=C)
        wout3 = phi[:, 0:3 * HID * C].rearrange("p (n k) -> p n k", n=C)
        ksb = sb("ksb", [P, D])
        wqbd = ksb[:, :].rearrange("p (c n) -> p c n", c=C)
        wkb = sb("wkb", [P, D])
        wkbd = wkb[:, :].rearrange("p (c n) -> p c n", c=C)
        bias_b = wkb
        wvbd = sb("wvbd", [P, C, P])
        kvn = xn[:, :].rearrange("p (c n) -> p c n", c=C)
        kvnT = xn2[:, :].rearrange("p (c n) -> p c n", c=C)
        kvT = phi[:, :].rearrange("p (c n) -> p c n", c=C)

        pool_cell = sb("pool_cell", [1, 2])
        dve_cell = sb("dve_cell", [1, 2])
        ident = sb("ident", [P, P])
        ones = sb("ones", [P, P])
        below = sb("below", [P, P])
        bdmask = sb("bdmask", [P, P])
        same = sb("same", [P, P])
        same_t = sb("same_t", [P, P])
        iota_i = sb("iota_i", [P, P], I32)
        iota_f = sb("iota_f", [P, P])
        dump_f = sb("dump_f", [P, 1])
        dump_i = sb("dump_i", [P, 1], I32)
        src_i = sb("src_i", [P, ET], I32)
        dst_i = sb("dst_i", [P, ET], I32)
        src_f = sb("src_f", [P, ET])
        ab_i = sb("ab_i", [P, 2, ET], I32)
        ab_f = sb("ab_f", [P, 2, ET])
        dis = sb("dis", [P, NT])
        disT = sb("disT", [NT, P])
        dis_src = sb("dis_src", [P, ET])
        dis_dst = sb("dis_dst", [P, ET])
        norm = sb("norm", [P, ET])
        rowsum = sb("rowsum", [P, NT])
        dis2 = sb("dis2", [P, NT])
        mhalf = sb("mhalf", [P, NT])
        stats = sb("stats", [P, 2, 6])
        mv = [sb(f"mv_slot{s}", [P, 2]) for s in range(RING)]
        mvt = sb("mvt", [P, NT, 2])
        nb = sb("nb", [P, NT])
        e_dst = sb("e_dst", [P, 1], I32)
        e_idx = sb("e_idx", [P, 1], I32)
        e_sc = sb("e_sc", [P, 8])
        e_stats = sb("e_stats", [P, 2, 6])
        e_mv = sb("e_mv", [P, 2])
        ks = sb("ks", [P, 9])
        rk = sb("rk", [P, 9])
        mx = sb("mx", [P, 2])
        row = sb("row", [1, 4])
        sc = sb("sc", [P, 8])
        s_w, s_m, s_t, s_y, s_a, t_inv, tmp0, tmp1 = [sc[:, k:k + 1] for k in range(8)]
        z16 = sb("z16", [P, H])
        stats2 = sb("stats2", [P, 2, 6])
        mv2 = sb("mv2", [P, 2])
        gbias = sb("gbias", [P, NGRP + NEXP])
        pen_a = sb("pen_a", [P, NEXP])
        pen_b = sb("pen_b", [P, NEXP])
        tri = sb("tri", [P, NEXP, NEXP])
        lg = sb("lg", [P, NGRP + NEXP])
        gs = sb("gs", [P, 8])
        v8 = sb("v8", [P, NEXP])
        NSIL = 2 * HID
        exb = sb("exb", [P, 1 + NSIL + NEXP])
        rec = sb("rec", [P, 1 + NSIL])
        hs = sb("hs", [P, NSIL])
        gt = sb("gt", [P, NEXP, NEXP])
        eq = sb("eq", [P, NEXP, NEXP])
        rank = sb("rank", [P, NEXP])
        hw = sb("hw", [P, NEXP, HID])
        sh3 = sb("sh3", [P, 3 * HID], F32R)

        ps = ctx.enter_context(nc.psum_tensor("ps", [P, 8, HALF], F32))

        def bank(b):
            return ps[:, b, :]

        idx_loaded = sem("idx_loaded")
        srcb_loaded = sem("srcb_loaded")
        w_loaded = sem("w_loaded")
        bd_loaded = sem("bd_loaded")
        ffn_loaded = sem("ffn_loaded")
        wo_loaded = sem("wo_loaded")
        bias_loaded = sem("bias_loaded")
        consts = sem("consts")
        consts_dve = sem("consts_dve")
        prep_dve = sem("prep_dve")
        prep_pe = sem("prep_pe")
        prep_pool = sem("prep_pool")
        dis_stored = sem("dis_stored")
        dis_gathered = sem("dis_gathered")
        job_done = sem("job_done")
        job_hi = sem("job_hi")
        job_lo = sem("job_lo")
        wq_split = sem("wq_split")
        agg_zeroed = sem("agg_zeroed")
        agg_added = sem("agg_added")
        x1_loaded = [sem(f"x1_loaded{s}") for s in range(RING)]
        stats1_done = sem("stats1_done")
        var1_ready = sem("var1_ready")
        rstd1_ready = sem("rstd1_ready")
        mv_kept = sem("mv_kept")
        xn1_ready = sem("xn1_ready")
        x1_turned = sem("x1_turned")
        x1T_ready = sem("x1T_ready")
        k_done = sem("k_done")
        kexp_done = sem("kexp_done")
        k_neg, q_neg = sem("k_neg"), sem("q_neg")
        phik_ready = sem("phik_ready")
        kv_done = sem("kv_done")
        e_cols = sem("e_cols")
        e_chain = sem("e_chain")
        e_gathered = sem("e_gathered")
        e_rstd = sem("e_rstd")
        e_summed = sem("e_summed")
        e_out = sem("e_out")
        e_carried = sem("e_carried")
        mid_dve = sem("mid_dve")
        mid_pe = sem("mid_pe")
        mid_act = sem("mid_act")
        m_done = sem("m_done")
        m_hi_done = sem("m_hi_done")
        m_lo_done = sem("m_lo_done")
        x2_loaded = [sem(f"x2_loaded{s}") for s in range(RING)]
        g_loaded = [sem(f"g_loaded{s}") for s in range(RING)]
        stored = [sem(f"stored{s}") for s in range(RING)]
        xn_ready = sem("xn_ready")
        y_ready = sem("y_ready")
        a_ready = sem("a_ready")
        xn2_ready = sem("xn2_ready")
        x_turned, x_hi, x_lo = sem("x_turned"), sem("x_hi"), sem("x_lo")
        y_turned, y_hi, y_lo = sem("y_turned"), sem("y_hi"), sem("y_lo")
        a_turned, a_hi, a_lo = sem("a_turned"), sem("a_hi"), sem("a_lo")
        n_turned, n_hi, n_lo = sem("n_turned"), sem("n_hi"), sem("n_lo")
        h_turned, h_hi, h_lo = sem("h_turned"), sem("h_hi"), sem("h_lo")
        q_done = sem("q_done")
        qexp_done = sem("qexp_done")
        phiq_ready = sem("phiq_ready")
        phik_scaled = sem("phik_scaled")
        z_chain = sem("z_chain")
        mix_done = sem("mix_done")
        mix_read = sem("mix_read")
        xp_ready = sem("xp_ready")
        ln2_chain = sem("ln2_chain")
        rstd2_ready = sem("rstd2_ready")
        fin_done = sem("fin_done")
        gate_chain = sem("gate_chain")
        gate_exp = sem("gate_exp")
        ffn_done = sem("ffn_done")
        out_ready = sem("out_ready")

        block = ctx.enter_context(nc.Block())

        def rows_of(t):
            if t.i is None and t.base == NTF:
                return slice(NTF * P, N), REM
            return (bass.ds(t.n * P, P) if t.i is not None else slice(t.base * P, (t.base + 1) * P)), P

        def walk1(eng, step, edge):
            for t in range(P1_FIRST):
                step(Tile(t))
            with eng.Fori(0, P1_A) as i:
                for u in range(RING):
                    step(Tile(P1_FIRST + u, i))
            first = P1_FIRST + RING * P1_A
            for u in range(RING):
                edge(0, u)
                step(Tile(first + u))
            edge(0, RING)
            with eng.Fori(1, ET) as i:
                for u in range(RING):
                    edge(i, u)
                    step(Tile(first + u, i))
                edge(i, RING)
            for t in range(first + RING * ET, NT):
                step(Tile(t))

        def walk2(eng, step):
            for t in range(-1, P2_FIRST):
                step(Tile(t))
            with eng.Fori(0, P2_TURNS) as i:
                for u in range(RING):
                    step(Tile(P2_FIRST + u, i))
            for t in range(P2_FIRST + RING * P2_TURNS, NT + 2):
                step(Tile(t))

        JOBS = ([("w", c, h) for c in range(C) for h in range(2)] + [("fin", c, 0) for c in range(C)]
                + [("wo", 0, h) for h in range(2)] + [("w2", g, h) for g in range(NGRP) for h in range(2)])
        NCONST = 10
        BD = 6
        PREP_HOT, PREP_DEG, PREP_DIST, PREP_MAX, PREP_POW, PREP_SCALE, PREP_OHN = 8, 9, 10, 11, 16, 17, 20
        MID_KVN, MID_MAX, MID_ROW, MID_SCALE, MID_ALL = 13, 23, 30, 31, 40
        GATE_EXP, GATE_N = 9, 27

        @block.sync
        def _(sp):
            sp.wait_ge(consts, NCONST)
            sp.dma_start(src_i[0:EP, :], src.rearrange("(p t) -> p t", t=ET)).then_inc(idx_loaded, 16)
            sp.dma_start(dst_i[0:EP, :], dst.rearrange("(p t) -> p t", t=ET)).then_inc(idx_loaded, 16)
            sp.dma_start(srcb[:, 0:EP, :], src.rearrange("(p t) -> p t", t=ET).partition_broadcast(P))\
              .then_inc(srcb_loaded, 16)
            sp.dma_start(wrows, gnn_W.rearrange("(o p) i -> p o i", p=P)).then_inc(w_loaded, 16)
            for w, t in ((Wq, wqbd), (Wk, wkbd), (Wv, wvbd[:, :, :])):
                two = w.rearrange("(c i) d e -> i d c e", i=2)
                for k in range(2):
                    sp.dma_start(t[k * DH:(k + 1) * DH, :, k * DH:(k + 1) * DH], two[k]).then_inc(bd_loaded, 16)

            def load1(t):
                r, n = rows_of(t)
                sp.dma_start(xin[t.slot][0:n, :], x[r, :]).then_inc(x1_loaded[t.slot], 16)

            for t in range(RING):
                load1(Tile(t))
            sp.dma_start(wcat1[0:2 * HID, :], w_in).then_inc(ffn_loaded, 16)
            sp.dma_start(wcat1[2 * HID:4 * HID, :], w1).then_inc(ffn_loaded, 16)
            sp.dma_start(wcat2[0:NGRP, :], wg).then_inc(ffn_loaded, 16)
            sp.dma_start(wcat2[NGRP:, :], we).then_inc(ffn_loaded, 16)
            for k in range(3):
                sp.dma_start(wout3[:, :, k * HID:(k + 1) * HID],
                             w_out.rearrange("(n p) h -> p n h", p=P)).then_inc(ffn_loaded, 16)
            for e in range(NEXP):
                sp.dma_start(w2rows[:, :, e, :], w2[e].rearrange("(n p) h -> p n h", p=P)).then_inc(ffn_loaded, 16)
            sp.dma_start(gbias[:, 0:NGRP], gb.partition_broadcast(P)).then_inc(ffn_loaded, 16)
            sp.dma_start(gbias[:, NGRP:], eb.partition_broadcast(P)).then_inc(ffn_loaded, 16)
            sp.wait_ge(prep_dve, PREP_DIST)
            sp.dma_start(dis_rows, disT[:, :]).then_inc(dis_stored, 16)
            sp.wait_ge(job_done, 2 * C)
            sp.dma_start(worows, Wo.rearrange("(c p) n -> p c n", p=P)).then_inc(wo_loaded, 16)

            def step(t):
                if (t + RING).within(NT):
                    sp.wait_ge(xn1_ready, count_of(t, 1, 1))
                    load1(t + RING)

            def edge(i, part):
                pass

            walk1(sp, step, edge)

            sp.wait_ge(k_done, 2 * NT)
            sp.dma_start(bias_b[:, :], gnn_b.partition_broadcast(P)).then_inc(bias_loaded, 16)

            def load2(t):
                r, n = rows_of(t)
                sp.dma_start(xin[t.slot][0:n, :], x[r, :]).then_inc(x2_loaded[t.slot], 16)
                sp.dma_start(gin[t.slot][0:n, :], agg[r, :]).then_inc(g_loaded[t.slot], 16)

            sp.wait_ge(xn1_ready, NT)
            sp.wait_ge(agg_zeroed, 16 * ZPARTS)
            sp.wait_ge(agg_added, 16 * ET)
            load2(Tile(0))

            def step(t):
                if (t + 2).within(NT):
                    wait(sp, xp_ready, count_of(t - 1, 2, 2))
                    wait(sp, y_turned, count_of(t - 1, 2, 2))
                    if t.base == 0:
                        sp.wait_ge(mid_pe, 5)
                    load2(t + 2)
                if (t - 2).within(NT):
                    sp.wait_ge(out_ready, count_of(t - 2, 2, 2))
                    r, n = rows_of(t - 2)
                    sp.dma_start(out[r, :], xp[(t - 2).slot][0:n, :]).then_inc(stored[(t - 2).slot], 16)

            walk2(sp, step)
            for s in range(RING):
                sp.wait_ge(stored[s], 16 * len(range(s, NT, RING)))

        @block.gpsimd
        def _(pool):
            pool.memset(src_i[:, :], PAD_SRC).then_inc(consts, 1)
            pool.memset(dst_i[:, :], 0).then_inc(consts, 1)
            pool.memset(srcb, PAD_SRC).then_inc(consts, 1)
            pool.memset(wqbd, 0.0).then_inc(consts, 1)
            pool.memset(wkbd, 0.0).then_inc(consts, 1)
            pool.memset(wvbd[:, :, :], 0.0).then_inc(consts, 1)
            pool.memset(ident[:, :], 0.0).then_inc(consts, 1)
            pool.memset(below[:, :], 1.0).then_inc(consts, 1)
            pool.memset(tri[:, :, :], 1.0).then_inc(consts, 1)
            pool.memset(pool_cell[:, :], 0.0).then_inc(consts, 1)
            pool.wait_ge(consts, NCONST)
            pool.affine_select(out=ident[:, :], in_=ident[:, :], compare_op=ALU.not_equal, fill=1.0, base=0,
                               pattern=[[-1, P]], channel_multiplier=1).then_inc(prep_pool, 1)
            pool.iota(iota_i[:, :], pattern=[[1, P]], base=0, channel_multiplier=0).then_inc(prep_pool, 1)
            pool.iota(dump_i[:, :], pattern=[[0, 1]], base=NT * P, channel_multiplier=1).then_inc(prep_pool, 1)
            pool.affine_select(out=below[:, :], in_=below[:, :], compare_op=ALU.is_gt, fill=0.0, base=0,
                               pattern=[[-1, P]], channel_multiplier=1).then_inc(prep_pool, 1)
            pool.affine_select(out=tri[:, :, :], in_=tri[:, :, :], compare_op=ALU.is_gt, fill=0.0, base=0,
                               pattern=[[1, NEXP], [-1, NEXP]], channel_multiplier=0).then_inc(prep_pool, 1)
            pool.memset(mhalf[:, :], -0.5).then_inc(prep_pool, 1)
            pool.wait_ge(prep_dve, PREP_DEG)
            pool.wait_ge(prep_pool, 6)
            pool.tensor_tensor(dis[:, :], dis[:, :], mhalf[:, :], ALU.pow).then_inc(prep_pool, 1)
            pool.wait_ge(dis_stored, 16)
            table = dis_rows.rearrange("t (p o) -> (t p) o", o=1)
            for k in range(ET):
                for idx, got in ((src_i, dis_src), (dst_i, dis_dst)):
                    pool.indirect_dma_start(
                        out=got[:, k:k + 1], out_offset=None, in_=table,
                        in_offset=bass.IndirectOffsetOnAxis(ap=idx[:, k:k + 1].bitcast(U32), axis=0),
                    ).then_inc(dis_gathered, 16)

            def rstd1(t):
                pool.wait_ge(var1_ready, count_of(t, 1, 1))
                m = mv[t.slot]
                pool.tensor_tensor(m[:, 1:2], m[:, 1:2], mhalf[:, 0:1], ALU.pow).then_inc(rstd1_ready, 1)
                pool.wait_ge(rstd1_ready, count_of(t, 1, 1))
                pool.tensor_copy(mvt[:, bass.ds(t.n, 1), :], m[:, None, :]).then_inc(mv_kept, 1)

            rstd1(Tile(0))
            rstd1(Tile(1))
            pool.wait_ge(job_done, len(JOBS))

            def step(t):
                if (t + 2).within(NT):
                    rstd1(t + 2)

            def edge(i, part):
                if part == 0:
                    pool.wait_ge(e_cols, i * 3 + 1)
                    wait(pool, e_summed, i * 2)
                    wait(pool, e_carried, i * 2)
                    carry(pool, pool_cell).then_inc(e_carried, 1)
                    pool.indirect_dma_start(
                        out=xe[:, :], out_offset=None, in_=x,
                        in_offset=bass.IndirectOffsetOnAxis(ap=e_dst[:, :].bitcast(U32), axis=0),
                    ).then_inc(e_gathered, 16)
                if part == 1:
                    pool.wait_ge(e_chain, i * 11 + 9)
                    pool.tensor_tensor(e_mv[:, 1:2], e_mv[:, 1:2], mhalf[:, 0:1], ALU.pow).then_inc(e_rstd, 1)
                if part == RING:
                    pool.wait_ge(e_out, i * 2 + 2)
                    pool.wait_ge(e_chain, i * 11 + 6)
                    wait(pool, agg_added, i * 16)
                    pool.wait_ge(agg_zeroed, 16 * ZPARTS)
                    pool.wait_ge(e_carried, i * 2 + 1)
                    carry(pool, pool_cell).then_inc(e_carried, 1)
                    pool.indirect_dma_start(
                        out=agg, out_offset=bass.IndirectOffsetOnAxis(ap=e_idx[:, :].bitcast(U32), axis=0),
                        in_=msum[:, :], in_offset=None, compute_op=ALU.add,
                    ).then_inc(agg_added, 16)

            walk1(pool, step, edge)

            def step(t):
                if (t - 1).within(NT):
                    pool.wait_ge(ln2_chain, count_of(t - 1, 3, 3))
                    pool.tensor_tensor(mv2[:, 1:2], mv2[:, 1:2], mhalf[:, 0:1], ALU.pow).then_inc(rstd2_ready, 1)
                if (t + 1).within(NT):
                    n = t + 1
                    if t.base == -1:
                        pool.wait_ge(mid_act, 6)
                    for h in range(2):
                        pool.wait_ge(phiq_ready, count_of(n, 2, h + 1))
                        e = phi[:, h * HALF:(h + 1) * HALF]
                        pool.tensor_tensor(e, e, ksb[:, h * HALF:(h + 1) * HALF], ALU.mult)\
                            .then_inc(phik_scaled, 1)
                    pool.wait_ge(z_chain, count_of(n, 3, 3))
                    p3 = phi[:, :].rearrange("p (h d) -> p h d", d=DH)
                    pool.tensor_tensor(p3, p3, z16[:, :, None].to_broadcast([P, H, DH]), ALU.mult)\
                        .then_inc(a_ready, 1)

            walk2(pool, step)

        @block.scalar
        def _(act):
            act.wait_ge(consts_dve, 1)
            act.wait_ge(w_loaded, 16)
            act.dma_start(agg[0:ZPREP * P, :].rearrange("(p a) d -> p a d", p=P),
                          zeros[:, None, :].to_broadcast([P, ZPREP, D])).then_inc(agg_zeroed, 16)
            act.wait_ge(prep_dve, PREP_SCALE)
            for j, (kind, c, h) in enumerate(JOBS):
                act.wait_ge(job_done, j + 1)
                b = bank(j % 2)
                if kind == "w":
                    o = act.activation(w_hi[:, c, h * HALF:(h + 1) * HALF], b, ACT.Copy, scale=s_w)
                elif kind == "fin":
                    o = act.activation(fin_hi[:, c, :], b[:, 0:FIN], ACT.Copy)
                elif kind == "wo":
                    o = act.activation(wo3[:, h * HALF:(h + 1) * HALF], b[0:3 * HID, :], ACT.Copy)
                else:
                    o = act.activation(w2_hi[:, c, h * HALF:(h + 1) * HALF], b, ACT.Copy)
                o.then_inc(job_hi, 1)

            def negative_exp(o, i, negated, done, count):
                act.activation(o, i, ACT.Relu, scale=-1.0).then_inc(negated, 1)
                act.wait_ge(negated, count)
                act.activation(o, o, ACT.Exp, scale=-1.0).then_inc(done, 1)

            def turn(t):
                for h in range(2):
                    act.wait_ge(x1_turned, count_of(t, 2, h + 1))
                    wait(act, k_done, count_of(t - 1, 2, h + 1))
                    act.activation(x1T[:, h * CH:(h + 1) * CH, :].rearrange("p c n -> p (c n)"), bank(h),
                                   ACT.Copy).then_inc(x1T_ready, 1)

            turn(Tile(0))

            def step(t):
                for h in range(2):
                    act.wait_ge(k_done, count_of(t, 2, h + 1))
                    wait(act, phik_ready, count_of(t - 1, 2, h + 1))
                    negative_exp(ex1[:, h * HALF:(h + 1) * HALF], bank(2 + h), k_neg, kexp_done, count_of(t, 2, h + 1))
                if (t + 1).within(NT):
                    turn(t + 1)
                if t.base < P1_BEFORE:
                    act.dma_start(agg[bass.ds((t.n * ZSTEP + ZPREP) * P, ZSTEP * P), :]
                                  .rearrange("(p a) d -> p a d", p=P),
                                  zeros[:, None, :].to_broadcast([P, ZSTEP, D])).then_inc(agg_zeroed, 16)

            def edge(i, part):
                if part == 2:
                    wait(act, agg_added, i * 16)
                    for h in range(2):
                        act.wait_ge(e_summed, i * 2 + 1 + h)
                        act.activation(msum[:, h * HALF:(h + 1) * HALF], bank(7), ACT.Copy).then_inc(e_out, 1)

            walk1(act, step, edge)

            act.wait_ge(mid_pe, 1)
            act.wait_ge(agg_added, 16 * ET)
            for h in range(2):
                act.activation(kvnT[:, h * CH:(h + 1) * CH, :].rearrange("p c n -> p (c n)"), bank(h),
                               ACT.Copy).then_inc(mid_act, 1)
            act.wait_ge(mid_pe, 2)
            for h in range(2):
                act.activation(kvT[:, h * CH:(h + 1) * CH, :].rearrange("p c n -> p (c n)"), bank(2 + h),
                               ACT.Copy).then_inc(mid_act, 1)
            act.wait_ge(mid_pe, 5)
            for h in range(2):
                act.activation(ksb[:, h * HALF:(h + 1) * HALF], bank(h), ACT.Copy).then_inc(mid_act, 1)
            act.wait_ge(mid_dve, MID_SCALE)
            for j in range(2 * C):
                act.wait_ge(m_done, j + 1)
                act.activation(m_hi[:, j // 2, (j % 2) * HALF:(j % 2 + 1) * HALF], bank(4 + j % 4), ACT.Copy,
                               scale=s_m).then_inc(m_hi_done, 1)

            def normalise(t):
                act.wait_ge(x2_loaded[t.slot], t.turn * 16 + 16)
                wait(act, x_turned, count_of(t - 1, 2, 2))
                wait(act, y_ready, count_of(t - 1, 1, 1))
                act.activation(xn[:, :], xin[t.slot][:, :], ACT.Identity, bias=nb[:, bass.ds(t.n, 1)],
                               scale=mvt[:, bass.ds(t.n, 1), 1:2].rearrange("p a b -> p (a b)"))\
                   .then_inc(xn_ready, 1)

            def high(t, turned, done, dest, scale=1.0):
                for h in range(2):
                    act.wait_ge(turned, count_of(t, 2, h + 1))
                    act.activation(dest[:, h * CH:(h + 1) * CH, :].rearrange("p c n -> p (c n)"), bank(h),
                                   ACT.Copy, scale=scale).then_inc(done, 1)

            act.wait_ge(mid_pe, 3)
            act.wait_ge(mid_dve, MID_ALL)
            normalise(Tile(0))

            def step(t):
                if (t - 2).within(NT):
                    act.wait_ge(h_turned, count_of(t - 2, 1, 1))
                    wait(act, ffn_done, count_of(t - 3, 2, 2))
                    act.activation(hwT_hi[:, :, :].rearrange("p c n -> p (c n)"), ps[:, 7, 0:2 * P], ACT.Copy)\
                       .then_inc(h_hi, 1)
                    act.activation(sh3T[:, :], ps[0:3 * HID, 7, 2 * P:3 * P], ACT.Copy).then_inc(h_hi, 1)
                if (t + 1).within(NT):
                    n = t + 1
                    wait(act, fin_done, count_of(t - 2, 1, 1))
                    high(n, x_turned, x_hi, fT_hi)
                    wait(act, a_turned, count_of(t, 2, 2))
                    for h in range(2):
                        act.wait_ge(q_done, count_of(n, 2, h + 1))
                        negative_exp(phi[:, h * HALF:(h + 1) * HALF], bank(2 + h), q_neg, qexp_done,
                                     count_of(n, 2, h + 1))
                if (t - 1).within(NT):
                    if not (t + 1).within(NT):
                        act.wait_ge(q_done, 2 * NT)
                    else:
                        act.wait_ge(q_done, count_of(t + 1, 2, 2))
                    high(t - 1, n_turned, n_hi, fT_hi)
                if (t + 1).within(NT):
                    n = t + 1
                    wait(act, mix_done, count_of(t - 2, 2, 2))
                    high(n, y_turned, y_hi, yT_hi[n.slot], s_y)
                if (t - 1).within(NT):
                    p = t - 1
                    act.wait_ge(gate_chain, count_of(p, GATE_N, GATE_EXP))
                    act.activation(exb[:, :], exb[:, :], ACT.Exp).then_inc(gate_exp, 1)
                if (t + 1).within(NT):
                    high(t + 1, a_turned, a_hi, aT_hi[(t + 1).slot], s_a)
                if (t + 2).within(NT):
                    normalise(t + 2)

            walk2(act, step)

        @block.tensor
        def _(pe):
            def wide(b, per, c):
                return bank(b)[:, c * per:(c + 1) * per]

            pe.wait_ge(consts_dve, 3)
            pe.wait_ge(prep_pool, 1)
            pe.wait_ge(prep_dve, PREP_HOT)
            for k in range(ET):
                mm = pe.matmul(bank(2)[:, 0:NT], ohb[:, k, :], oha[:, k, :], start=(k == 0), stop=(k == ET - 1))
            mm.then_inc(prep_pe, 1)
            pe.wait_ge(prep_pool, 7)
            pe.matmul(bank(2)[0:NT, 0:P], dis[:, :], ident[:, :], start=True, stop=True).then_inc(prep_pe, 1)
            pe.wait_ge(prep_dve, PREP_MAX)
            pe.matmul(bank(3)[0:1, 0:P], mx[:, 0:1], ident[:, :], start=True, stop=True).then_inc(prep_pe, 1)
            pe.wait_ge(prep_dve, PREP_POW)
            pe.matmul(bank(3)[:, 0:1], ones[0:1, :], row[0:1, 0:1], start=True, stop=True).then_inc(prep_pe, 1)
            pe.wait_ge(w_loaded, 16)
            for j, (kind, c, h) in enumerate(JOBS):
                if j >= 2:
                    pe.wait_ge(job_lo, j - 1)
                if j == 2 * C:
                    pe.wait_ge(ffn_loaded, 16 * (4 + 3 + NEXP + 2))
                if kind == "fin":
                    mm = pe.transpose(wide(j % 2, P, 0), wcat1[:, c * P:(c + 1) * P], ident[:, :])
                    mm = pe.matmul(bank(j % 2)[:, P:FIN], wcat2[:, c * P:(c + 1) * P],
                                   ident[0:NGRP + NEXP, 0:NGRP + NEXP], start=True, stop=True)
                else:
                    for k in range(4):
                        if kind == "w":
                            mm = pe.transpose(wide(j % 2, P, k), wrows[:, h * 4 + k, c * P:(c + 1) * P],
                                              ident[:, :])
                        elif kind == "wo":
                            mm = pe.matmul(bank(j % 2)[0:3 * HID, k * P:(k + 1) * P], wout3[:, h * 4 + k, :],
                                           ident[:, :], start=True, stop=True)
                        else:
                            mm = pe.transpose(
                                wide(j % 2, P, k),
                                w2rows[:, h * 4 + k, c * EPG:(c + 1) * EPG, :].rearrange("p e h -> p (e h)"),
                                ident[:, :])
                mm.then_inc(job_done, 1)

            for b in range(3):
                pe.matmul(bank(4 + b), zeros[:, 0:P], zeros[:, 0:HALF], start=True, stop=False,
                          skip_group_check=True)

            pe.wait_ge(prep_dve, PREP_OHN)
            for k in range(ET):
                mm = pe.matmul(bank(3)[:, 0:NT], ohb[:, k, :], ohn[:, k, :], start=(k == 0), stop=(k == ET - 1))
            mm.then_inc(prep_pe, 1)

            def turn(t):
                pe.wait_ge(xn1_ready, count_of(t, 1, 1))
                for h in range(2):
                    wait(pe, x1T_ready, count_of(t - 1, 2, h + 1))
                    for c in range(CH):
                        mm = pe.transpose(wide(h, P, c), xn1[t.slot][:, h * CH + c, 0:P], ident[:, :])
                    mm.then_inc(x1_turned, 1)

            def keyval(t, rows):
                pe.wait_ge(phik_ready, count_of(t, 2, 2))
                for c in range(C):
                    mm = pe.matmul(bank(4 + c // 3)[:, (c % 3) * (P + 1):(c % 3 + 1) * (P + 1)],
                                   phi1[t.slot][0:rows, c * P:(c + 1) * P], xn1[t.slot][0:rows, c, :],
                                   start=False, stop=False, skip_group_check=True)
                mm.then_inc(kv_done, 1)

            pe.wait_ge(job_lo, len(JOBS))
            pe.wait_ge(wq_split, 2)
            pe.wait_ge(bd_loaded, 16 * BD)
            turn(Tile(0))

            def step(t):
                for h in range(2):
                    pe.wait_ge(x1T_ready, count_of(t, 2, h + 1))
                    wait(pe, phik_ready, count_of(t - 1, 2, h + 1))
                    for c in range(CH):
                        mm = pe.matmul(wide(2 + h, P, c), x1T[:, h * CH + c, :], wkbd[:, h * CH + c, :],
                                       start=True, stop=True)
                    mm.then_inc(k_done, 1)
                if (t + 1).within(NT):
                    turn(t + 1)
                if (t - 1).within(NT):
                    keyval(t - 1, P)

            def edge(i, part):
                if part == 2:
                    pe.wait_ge(e_chain, i * 11 + 11)
                    for h in range(2):
                        wait(pe, e_out, i * 2 + h)
                        pe.matmul(bank(7), same[:, :], xe[:, h * HALF:(h + 1) * HALF], start=True, stop=True)\
                          .then_inc(e_summed, 1)

            walk1(pe, step, edge)
            keyval(Tile(NT - 1), REM)

            pe.wait_ge(mid_dve, MID_KVN)
            for c in range(C):
                mm = pe.transpose(wide(c // CH, P, c % CH), kvn[:, c, :], ident[:, :])
            mm.then_inc(mid_pe, 1)
            pe.wait_ge(mid_act, 2)
            for c in range(C):
                mm = pe.matmul(wide(2 + c // CH, P, c % CH), wvbd[:, c, :], kvnT[:, c, :], start=True, stop=True)
            mm.then_inc(mid_pe, 1)
            pe.wait_ge(mid_dve, MID_MAX)
            for k in range(2):
                mm = pe.matmul(bank(7)[0:1, k * P:(k + 1) * P], mx[:, k:k + 1], ident[:, :], start=True, stop=True)
            mm.then_inc(mid_pe, 1)
            pe.wait_ge(mid_dve, MID_ROW)
            pe.matmul(bank(7)[:, 0:1], ones[0:1, :], row[0:1, 0:1], start=True, stop=True).then_inc(mid_pe, 1)
            for c in range(C):
                mm = pe.matmul(wide(c // CH, P, c % CH), ones[:, :], dgm[:, c, :], start=True, stop=True)
            mm.then_inc(mid_pe, 1)
            pe.wait_ge(mid_act, 4)
            pe.wait_ge(wo_loaded, 16)
            for j in range(2 * C):
                if j >= 4:
                    pe.wait_ge(m_lo_done, j - 3)
                if j == 3:
                    pe.wait_ge(mid_dve, MID_SCALE)
                pe.matmul(bank(4 + j % 4), kvT[:, j // 2, :], worows[:, j // 2, (j % 2) * HALF:(j % 2 + 1) * HALF],
                          start=True, stop=True).then_inc(m_done, 1)

            def turn2(t, ready, what, turned, free, free_at):
                pe.wait_ge(ready, count_of(t, 1, 1))
                for h in range(2):
                    if free is not None:
                        wait(pe, free, free_at(h))
                    for c in range(CH):
                        mm = pe.transpose(wide(h, P, c), what[:, (h * CH + c) * P:(h * CH + c + 1) * P],
                                          ident[:, :])
                    mm.then_inc(turned, 1)

            def mix(t, part):
                h, quarter = part // 4, part % 4
                if quarter == 0:
                    wait(pe, mix_read, count_of(t - 1, 2, h + 1))
                    pe.wait_ge(y_lo, count_of(t, 2, 2))
                    if t.base == 0 and h == 0:
                        pe.wait_ge(m_lo_done, 2 * C)
                if quarter == 2:
                    pe.wait_ge(a_lo, count_of(t, 2, 2))
                s = t.slot
                hi, lo, u_hi, u_lo = ((yT_hi[s], yT_lo[s], w_hi, w_lo) if quarter < 2
                                      else (aT_hi[s], aT_lo[s], m_hi, m_lo))
                cols = slice(h * HALF, (h + 1) * HALF)
                for c in range((quarter % 2) * CH, (quarter % 2 + 1) * CH):
                    pe.matmul(bank(4 + h), hi[:, c, :], u_hi[:, c, cols], start=(quarter == 0 and c == 0),
                              stop=False)
                    pe.matmul(bank(4 + h), hi[:, c, :], u_lo[:, c, cols], start=False, stop=False)
                    mm = pe.matmul(bank(4 + h), lo[:, c, :], u_hi[:, c, cols], start=False,
                                   stop=(quarter == 3 and c == C - 1))
                if quarter == 3:
                    mm.then_inc(mix_done, 1)

            def thrice(o, l_hi, l_lo, r_hi, r_lo, start, stop):
                pe.matmul(o, l_hi, r_hi, start=start, stop=False)
                pe.matmul(o, l_hi, r_lo, start=False, stop=False)
                return pe.matmul(o, l_lo, r_hi, start=False, stop=stop)

            def step(t):
                now, prep, post, last = t.within(NT), (t + 1).within(NT), (t - 1).within(NT), (t - 2).within(NT)
                n, p, o = t + 1, t - 1, t - 2
                if now:
                    mix(t, 0)
                if last:
                    pe.wait_ge(gate_chain, count_of(o, GATE_N, GATE_N))
                    wait(pe, out_ready, count_of(t - 3, 2, 2))
                    for g in range(NGRP):
                        pe.transpose(ps[:, 7, g * P:(g + 1) * P],
                                     hw[:, g * EPG:(g + 1) * EPG, :].rearrange("p e h -> p (e h)"), ident[:, :])
                    pe.matmul(ps[0:3 * HID, 7, 2 * P:3 * P], sh3[:, :].bitcast(F32), ident[:, :],
                              start=True, stop=True).then_inc(h_turned, 1)
                if prep:
                    if t.base == -1:
                        pe.wait_ge(mid_act, 6)
                    turn2(n, xn_ready, xn, x_turned, a_lo, lambda h: count_of(t, 2, h + 1))
                if now:
                    mix(t, 1)
                if last:
                    pe.wait_ge(h_hi, count_of(o, 2, 2))
                    pe.wait_ge(h_lo, count_of(o, 1, 1))
                    for h in range(2):
                        cols = slice(h * HALF, (h + 1) * HALF)
                        for g in range(NGRP):
                            thrice(bank(6 + h), hwT_hi[:, g, :], hwT_lo[:, g, :], w2_hi[:, g, cols],
                                   w2_lo[:, g, cols], g == 0, False)
                        pe.matmul(bank(6 + h), sh3T[:, :], wo3[:, cols], start=False, stop=True)\
                          .then_inc(ffn_done, 1)
                if prep:
                    for h in range(2):
                        pe.wait_ge(x_lo, count_of(n, 2, h + 1))
                        wait(pe, phiq_ready, count_of(t, 2, h + 1))
                        for c in range(CH):
                            cc = h * CH + c
                            mm = thrice(wide(2 + h, P, c), fT_hi[:, cc, :], fT_lo[:, cc, :], wq_hi[:, cc, :],
                                        wq_lo[:, cc, :], True, True)
                        mm.then_inc(q_done, 1)
                if now:
                    mix(t, 2)
                if post:
                    free = (x_lo, lambda h: count_of(n, 2, h + 1)) if prep else (a_lo, lambda h: 2 * NT)
                    turn2(p, xn2_ready, xn2, n_turned, *free)
                if now:
                    mix(t, 3)
                if post:
                    pe.wait_ge(n_lo, count_of(p, 2, 2))
                    wait(pe, out_ready, count_of(t - 2, 2, 1))
                    for c in range(C):
                        mm = thrice(bank(6)[:, 0:FIN], fT_hi[:, c, :], fT_lo[:, c, :], fin_hi[:, c, :],
                                    fin_lo[:, c, :], c == 0, c == C - 1)
                    mm.then_inc(fin_done, 1)
                if prep:
                    free = ((n_lo, lambda h: count_of(p, 2, h + 1)) if post
                            else (x_lo, lambda h: count_of(n, 2, h + 1)))
                    turn2(n, y_ready, gin[n.slot], y_turned, *free)
                if now:
                    mix(t, 4)
                    mix(t, 5)
                if now:
                    mix(t, 6)
                if prep:
                    turn2(n, a_ready, phi, a_turned, y_lo, lambda h: count_of(n, 2, h + 1))
                if now:
                    mix(t, 7)

            walk2(pe, step)

        @block.vector
        def _(dve):
            def chain(s, start=0):
                state = [start]

                def do(inst):
                    inst.then_inc(s, 1)
                    state[0] = state[0] + 1
                    dve.wait_ge(s, state[0])
                return do, state

            dve.memset(zeros, 0.0).then_inc(consts_dve, 1)
            dve.memset(bdmask[:, :], 0.0).then_inc(consts_dve, 1)
            dve.memset(ones[:, :], 1.0).then_inc(consts_dve, 1)
            dve.wait_ge(consts_dve, 2)
            for k in range(2):
                dve.memset(bdmask[k * DH:(k + 1) * DH, k * DH:(k + 1) * DH], 1.0).then_inc(consts_dve, 1)
            dve.memset(pen_a[:, 0:EPG], -BIG).then_inc(consts_dve, 1)
            dve.memset(pen_a[:, EPG:], BIG).then_inc(consts_dve, 1)
            dve.memset(pen_b[:, 0:EPG], 0.0).then_inc(consts_dve, 1)
            dve.memset(pen_b[:, EPG:], -BIG).then_inc(consts_dve, 1)
            dve.memset(row[:, :], 0.0).then_inc(consts_dve, 1)
            dve.memset(dve_cell[:, :], 0.0).then_inc(consts_dve, 1)

            do, at = chain(prep_dve)
            dve.wait_ge(consts_dve, 11)
            dve.wait_ge(prep_pool, 6)
            dve.wait_ge(idx_loaded, 32)
            do(dve.tensor_copy(src_f[:, :], src_i[:, :]))
            do(dve.tensor_scalar(ab_i[:, 0, :], src_i[:, :], 7, None, ALU.logical_shift_right))
            do(dve.tensor_scalar(ab_i[:, 1, :], src_i[:, :], P - 1, None, ALU.bitwise_and))
            do(dve.tensor_copy(ab_f[:, :, :], ab_i[:, :, :]))
            do(dve.tensor_copy(iota_f[:, :], iota_i[:, :]))
            do(dve.tensor_copy(dump_f[:, :], dump_i[:, :]))
            do(dve.tensor_tensor(oha, iota_f[:, None, 0:NT].to_broadcast([P, ET, NT]),
                                 ab_f[:, 0, :, None].to_broadcast([P, ET, NT]), ALU.is_equal))
            do(dve.tensor_tensor(ohb, iota_f[:, None, :].to_broadcast([P, ET, P]),
                                 ab_f[:, 1, :, None].to_broadcast([P, ET, P]), ALU.is_equal))
            assert at[0] == PREP_HOT
            dve.wait_ge(prep_pe, 1)
            do(dve.tensor_scalar(dis[:, :], bank(2)[:, 0:NT], 1.0, None, ALU.add))
            assert at[0] == PREP_DEG
            dve.wait_ge(prep_pe, 2)
            do(dve.tensor_copy(disT[:, :], bank(2)[0:NT, 0:P]))
            assert at[0] == PREP_DIST

            def max_abs(o, i):
                return dve.tensor_reduce(o, i, AX_X, ALU.max, apply_absolute_value=True)

            def power_of_two(do, v, factor, top):
                do(dve.tensor_scalar(v, v, factor, 1e-25, ALU.mult, ALU.max))
                do(dve.reciprocal(v, v))
                do(dve.tensor_scalar(v, v, top, None, ALU.mult))
                do(dve.tensor_scalar(v.bitcast(I32), v.bitcast(I32), 0x7F800000, None, ALU.bitwise_and))

            dve.wait_ge(w_loaded, 16)
            do(max_abs(mx[:, 0:1], wrows.rearrange("p o i -> p (o i)")))
            assert at[0] == PREP_MAX
            dve.wait_ge(prep_pe, 3)
            do(dve.tensor_reduce(row[0:1, 0:1], bank(3)[0:1, 0:P], AX_X, ALU.max))
            power_of_two(do, row[0:1, 0:1], 1.0, W_TOP)
            assert at[0] == PREP_POW
            dve.wait_ge(prep_pe, 4)
            do(dve.tensor_copy(s_w, bank(3)[:, 0:1]))
            assert at[0] == PREP_SCALE

            for j, (kind, c, h) in enumerate(JOBS):
                dve.wait_ge(job_hi, j + 1)
                b = bank(j % 2)
                cols = slice(h * HALF, (h + 1) * HALF)
                if kind == "w":
                    o = dve.scalar_tensor_tensor(w_lo[:, c, cols], b, s_w, w_hi[:, c, cols], ALU.mult, ALU.subtract)
                elif kind == "fin":
                    o = dve.tensor_tensor(fin_lo[:, c, :], b[:, 0:FIN], fin_hi[:, c, :].bitcast(F32), ALU.subtract)
                elif kind == "wo":
                    third = wo3[2 * HID:3 * HID, cols]
                    o = dve.tensor_tensor(third, b[2 * HID:3 * HID, :], third.bitcast(F32), ALU.subtract)
                else:
                    o = dve.tensor_tensor(w2_lo[:, c, cols], b, w2_hi[:, c, cols].bitcast(F32), ALU.subtract)
                o.then_inc(job_lo, 1)
            dve.wait_ge(bd_loaded, 16 * BD)
            dve.tensor_copy(wq_hi[:, :, :], wqbd).then_inc(wq_split, 1)
            dve.wait_ge(wq_split, 1)
            dve.tensor_tensor(wq_lo[:, :, :], wqbd, wq_hi[:, :, :].bitcast(F32), ALU.subtract).then_inc(wq_split, 1)

            dve.wait_ge(dis_gathered, 16 * 2 * ET)
            do(dve.tensor_tensor(norm[:, :], dis_src[:, :], dis_dst[:, :], ALU.mult))
            do(dve.tensor_tensor(dis2[:, :], dis[:, :], dis[:, :], ALU.mult))
            do(dve.tensor_tensor(ohn, oha, norm[:, :, None].to_broadcast([P, ET, NT]), ALU.mult))
            assert at[0] == PREP_OHN
            dve.wait_ge(prep_pe, 5)
            do(dve.tensor_tensor(rowsum[:, :], bank(3)[:, 0:NT], dis2[:, :], ALU.add))
            for s in range(RING):
                do(dve.memset(xn1[s][:, :, P:P + 1], 1.0))

            def statistics(t):
                dve.wait_ge(x1_loaded[t.slot], t.turn * 16 + 16)
                wait(dve, mv_kept, count_of(t - RING, 1, 1))
                for h in range(2):
                    o = dve.bn_stats(stats[:, h, :], xin[t.slot][:, h * HALF:(h + 1) * HALF])
                m = mv[t.slot]
                o.then_inc(stats1_done, 1)
                dve.wait_ge(stats1_done, count_of(t, 2, 1))
                carry(dve, dve_cell)
                dve.bn_aggr(m[:, :], stats[:, :, :]).then_inc(stats1_done, 1)
                dve.wait_ge(stats1_done, count_of(t, 2, 2))
                dve.tensor_scalar(m[:, 1:2], m[:, 1:2], LN_EPS, None, ALU.add).then_inc(var1_ready, 1)

            def normal(t):
                dve.wait_ge(rstd1_ready, count_of(t, 1, 1))
                wait(dve, kv_done, count_of(t - RING, 1, 1))
                m = mv[t.slot]
                dve.tensor_scalar(xn1[t.slot][:, :, 0:P], xin[t.slot][:, :].rearrange("p (c f) -> p c f", c=C),
                                  m[:, 0:1], m[:, 1:2], ALU.subtract, ALU.mult).then_inc(xn1_ready, 1)

            statistics(Tile(0))
            statistics(Tile(1))
            normal(Tile(0))

            def step(t):
                if (t + 2).within(NT):
                    statistics(t + 2)
                if (t + 1).within(NT):
                    normal(t + 1)
                for h in range(2):
                    cols = slice(h * HALF, (h + 1) * HALF)
                    dve.wait_ge(kexp_done, count_of(t, 2, h + 1))
                    dve.scalar_tensor_tensor(phi1[t.slot][:, cols], bank(2 + h), 0.0, ex1[:, cols], ALU.max, ALU.add)\
                       .then_inc(phik_ready, 1)

            def edge(i, part):
                def col(k):
                    return e_sc[:, k:k + 1]

                src_c, norm_c, dup_c, gap_c, rn_c = [col(k) for k in range(5)]
                if part == 0:
                    one = bass.ds(i, 1)
                    dve.tensor_copy(e_dst[:, :], dst_i[:, one]).then_inc(e_cols, 1)
                    dve.tensor_copy(src_c, src_f[:, one]).then_inc(e_cols, 1)
                    dve.tensor_copy(norm_c, norm[:, one]).then_inc(e_cols, 1)
                    dve.wait_ge(e_cols, i * 3 + 3)
                    wait(dve, e_summed, i * 2)
                    do, _ = chain(e_chain, i * 11)
                    do(dve.tensor_scalar(same[:, :], srcb[:, :, one].rearrange("p e o -> p (e o)"), src_c, None,
                                         ALU.is_equal))
                    do(dve.tensor_tensor(same_t[:, :], same[:, :], below[:, :], ALU.mult))
                    do(dve.tensor_reduce(dup_c, same_t[:, :], AX_X, ALU.add))
                    do(dve.tensor_scalar(dup_c, dup_c, 1.0, None, ALU.min))
                    do(dve.tensor_scalar(gap_c, dump_f[:, :], src_c, None, ALU.subtract))
                    wait(dve, agg_added, i * 16)
                    do(dve.tensor_scalar(e_idx[:, :], dup_c, gap_c, src_c, ALU.mult, ALU.add))
                if part == 1:
                    dve.wait_ge(e_gathered, i * 16 + 16)
                    do, _ = chain(e_chain, i * 11 + 6)
                    dve.bn_stats(e_stats[:, 0, :], xe[:, 0:HALF])
                    do(dve.bn_stats(e_stats[:, 1, :], xe[:, HALF:D]))
                    carry(dve, dve_cell)
                    do(dve.bn_aggr(e_mv[:, :], e_stats[:, :, :]))
                    do(dve.tensor_scalar(e_mv[:, 1:2], e_mv[:, 1:2], LN_EPS, None, ALU.add))
                if part == 2:
                    dve.wait_ge(e_rstd, i + 1)
                    do, _ = chain(e_chain, i * 11 + 9)
                    do(dve.tensor_tensor(rn_c, e_mv[:, 1:2], norm_c, ALU.mult))
                    do(dve.tensor_scalar(xe[:, :], xe[:, :], e_mv[:, 0:1], rn_c, ALU.subtract, ALU.mult))

            dve.wait_ge(srcb_loaded, 16)
            walk1(dve, step, edge)

            do, at = chain(mid_dve)
            dve.wait_ge(kv_done, NT)
            for b in range(3):
                do(dve.tensor_copy(ks[:, 3 * b:3 * b + (3 if b < 2 else 2)],
                                   bank(4 + b)[:, P:(3 if b < 2 else 2) * (P + 1):P + 1]))
            do(dve.tensor_scalar(rk[:, 0:C], ks[:, 0:C], 1e-37, None, ALU.max))
            do(dve.reciprocal(rk[:, 0:C], rk[:, 0:C]))
            for c in range(C):
                do(dve.scalar_tensor_tensor(kvn[:, c, :], bank(4 + c // 3)[:, (c % 3) * (P + 1):(c % 3) * (P + 1) + P],
                                            rk[:, c:c + 1], bdmask[:, :], ALU.mult, ALU.mult))
            assert at[0] == MID_KVN
            for c in range(C):
                do(dve.tensor_scalar(dgm[:, c, :], ident[:, :], ks[:, c:c + 1], None, ALU.mult))
            dve.wait_ge(mid_act, 4)
            do(max_abs(mx[:, 0:1], phi[:, :]))
            dve.wait_ge(wo_loaded, 16)
            do(max_abs(mx[:, 1:2], worows.rearrange("p c n -> p (c n)")))
            assert at[0] == MID_MAX
            dve.wait_ge(mid_pe, 3)
            for k in range(2):
                do(dve.tensor_reduce(row[0:1, k:k + 1], bank(7)[0:1, k * P:(k + 1) * P], AX_X, ALU.max))
            do(dve.tensor_tensor(row[0:1, 0:1], row[0:1, 0:1], row[0:1, 1:2], ALU.mult))
            power_of_two(do, row[0:1, 0:1], float(DH), W_TOP)
            assert at[0] == MID_ROW
            dve.wait_ge(mid_pe, 4)
            do(dve.tensor_copy(s_m, bank(7)[:, 0:1]))
            assert at[0] == MID_SCALE
            do(dve.tensor_scalar(tmp0, s_w, Y_SCALE_MAX, None, ALU.mult))
            do(dve.tensor_scalar(tmp1, s_m, A_SCALE_MAX, None, ALU.mult))
            do(dve.tensor_tensor(s_t, tmp0, tmp1, ALU.min))
            do(dve.reciprocal(t_inv, s_t))
            do(dve.reciprocal(tmp0, s_w))
            do(dve.tensor_tensor(s_y, s_t, tmp0, ALU.mult))
            do(dve.reciprocal(tmp1, s_m))
            do(dve.tensor_tensor(s_a, s_t, tmp1, ALU.mult))
            dve.wait_ge(mv_kept, NT)
            do(dve.scalar_tensor_tensor(nb[:, :], mvt[:, :, 0], -1.0, mvt[:, :, 1], ALU.mult, ALU.mult))
            assert at[0] == MID_ALL
            for j in range(2 * C):
                dve.wait_ge(m_hi_done, j + 1)
                cols = slice((j % 2) * HALF, (j % 2 + 1) * HALF)
                dve.scalar_tensor_tensor(m_lo[:, j // 2, cols], bank(4 + j % 4), s_m, m_hi[:, j // 2, cols],
                                         ALU.mult, ALU.subtract).then_inc(m_lo_done, 1)

            dve.wait_ge(bias_loaded, 16)

            def low(t, hi_done, done, hi, lo, scale=None):
                for h in range(2):
                    dve.wait_ge(hi_done, count_of(t, 2, h + 1))
                    o = lo[:, h * CH:(h + 1) * CH, :].rearrange("p c n -> p (c n)")
                    g = hi[:, h * CH:(h + 1) * CH, :].rearrange("p c n -> p (c n)")
                    if scale is None:
                        i = dve.tensor_tensor(o, bank(h), g.bitcast(F32), ALU.subtract)
                    else:
                        i = dve.scalar_tensor_tensor(o, bank(h), scale, g, ALU.mult, ALU.subtract)
                    i.then_inc(done, 1)

            def mixed(t, h):
                cols = slice(h * HALF, (h + 1) * HALF)
                x_ = xp[t.slot][:, cols]
                dve.wait_ge(mix_done, count_of(t, 2, h + 1))
                if t.i is not None or t.turn >= 1:
                    dve.wait_ge(stored[t.slot], t.turn * 16)
                dve.scalar_tensor_tensor(x_, bank(4 + h), t_inv, xin[t.slot][:, cols], ALU.mult, ALU.add)\
                   .then_inc(mix_read, 1)
                dve.wait_ge(mix_read, count_of(t, 2, h + 1))
                dve.scalar_tensor_tensor(x_, bias_b[:, cols], rowsum[:, bass.ds(t.n, 1)], x_, ALU.mult, ALU.add)\
                   .then_inc(xp_ready, 1)
                dve.wait_ge(xp_ready, count_of(t, 2, h + 1))
                return dve.bn_stats(stats2[:, h, :], x_)

            def gate_in(p):
                do, at = chain(gate_chain, count_of(p, GATE_N, 0))
                f = bank(6)
                dve.wait_ge(fin_done, count_of(p, 1, 1))
                do(dve.tensor_tensor(lg[:, :], f[:, 4 * HID:FIN], gbias[:, :], ALU.add))
                do(dve.tensor_scalar(gs[:, 0:1], lg[:, 1:2], lg[:, 0:1], None, ALU.subtract))
                do(dve.tensor_scalar(gs[:, 1:2], gs[:, 0:1], 0.0, None, ALU.is_gt))
                do(dve.scalar_tensor_tensor(exb[:, 0:1], gs[:, 0:1], -1.0, gs[:, 0:1], ALU.mult, ALU.min))
                do(dve.scalar_tensor_tensor(v8[:, :], pen_a[:, :], gs[:, 1:2], pen_b[:, :], ALU.mult, ALU.add))
                do(dve.tensor_tensor(v8[:, :], v8[:, :], lg[:, NGRP:], ALU.add))
                do(dve.tensor_reduce(gs[:, 2:3], v8[:, :], AX_X, ALU.max))
                do(dve.tensor_scalar(exb[:, 1 + NSIL:], v8[:, :], gs[:, 2:3], None, ALU.subtract))
                do(dve.tensor_scalar(exb[:, 1:1 + NSIL].rearrange("p (k h) -> p k h", k=2),
                                     f[:, 0:4 * HID].rearrange("p (k h) -> p k h", k=2)[:, :, 0:HID],
                                     -1.0, 80.0, ALU.mult, ALU.min))

            def gate_out(p):
                do, at = chain(gate_chain, count_of(p, GATE_N, GATE_EXP))
                ab = bank(6)[:, 0:4 * HID].rearrange("p (k h) -> p k h", k=2)
                hs2 = hs[:, :].rearrange("p (k h) -> p k h", k=2)
                pe8 = exb[:, 1 + NSIL:]
                dve.wait_ge(gate_exp, count_of(p, 1, 1))
                do(dve.tensor_scalar(rec[:, :], exb[:, 0:1 + NSIL], 1.0, None, ALU.add))
                do(dve.reciprocal(rec[:, :], rec[:, :]))
                do(dve.tensor_tensor(hs2, ab[:, :, 0:HID], rec[:, 1:].rearrange("p (k h) -> p k h", k=2), ALU.mult))
                do(dve.tensor_tensor(hs2, ab[:, :, HID:2 * HID], hs2, ALU.mult))
                other = pe8[:, None, :].to_broadcast([P, NEXP, NEXP])
                mine = pe8[:, :, None].to_broadcast([P, NEXP, NEXP])
                do(dve.tensor_tensor(gt[:, :, :], other, mine, ALU.is_gt))
                do(dve.tensor_tensor(eq[:, :, :], other, mine, ALU.is_equal))
                do(dve.tensor_tensor(eq[:, :, :], eq[:, :, :], tri[:, :, :], ALU.mult))
                do(dve.tensor_tensor(gt[:, :, :], gt[:, :, :], eq[:, :, :], ALU.add))
                do(dve.tensor_reduce(rank[:, :], gt[:, :, :], AX_X, ALU.add))
                do(dve.scalar_tensor_tensor(rank[:, :], rank[:, :], 2.0, pe8, ALU.is_lt, ALU.mult))
                do(dve.tensor_reduce(gs[:, 3:4], pe8, AX_X, ALU.add))
                do(dve.reciprocal(gs[:, 4:5], gs[:, 3:4]))
                do(dve.tensor_tensor(gs[:, 5:6], gs[:, 4:5], rec[:, 0:1], ALU.mult))
                do(dve.tensor_scalar(rank[:, :], rank[:, :], gs[:, 5:6], None, ALU.mult))
                wait(dve, h_turned, count_of(p - 1, 1, 1))
                do(dve.tensor_tensor(hw[:, :, :], hs[:, None, HID:].to_broadcast([P, NEXP, HID]),
                                     rank[:, :, None].to_broadcast([P, NEXP, HID]), ALU.mult))
                do(dve.tensor_copy(sh3[:, 0:HID], hs[:, 0:HID]))
                do(dve.tensor_tensor(sh3[:, HID:2 * HID], hs[:, 0:HID], sh3[:, 0:HID].bitcast(F32), ALU.subtract))
                do(dve.tensor_copy(sh3[:, 2 * HID:], hs[:, 0:HID]))

            def step(t):
                now, prep, post = t.within(NT), (t + 1).within(NT), (t - 1).within(NT)
                n, p = t + 1, t - 1
                if post:
                    mixed(p, 1).then_inc(ln2_chain, 1)
                    dve.wait_ge(ln2_chain, count_of(p, 3, 1))
                    carry(dve, dve_cell)
                    dve.bn_aggr(mv2[:, :], stats2[:, :, :]).then_inc(ln2_chain, 1)
                    dve.wait_ge(ln2_chain, count_of(p, 3, 2))
                    dve.tensor_scalar(mv2[:, 1:2], mv2[:, 1:2], LN_EPS, None, ALU.add).then_inc(ln2_chain, 1)
                if (t - 2).within(NT):
                    dve.wait_ge(h_hi, count_of(t - 2, 2, 2))
                    dve.tensor_tensor(hwT_lo[:, :, :].rearrange("p c n -> p (c n)"), ps[:, 7, 0:2 * P],
                                      hwT_hi[:, :, :].rearrange("p c n -> p (c n)").bitcast(F32), ALU.subtract)\
                       .then_inc(h_lo, 1)
                if prep:
                    low(n, x_hi, x_lo, fT_hi, fT_lo)
                if post:
                    dve.wait_ge(rstd2_ready, count_of(p, 1, 1))
                    wait(dve, n_turned, count_of(t - 2, 2, 2))
                    dve.tensor_scalar(xn2[:, :], xp[p.slot][:, :], mv2[:, 0:1], mv2[:, 1:2], ALU.subtract,
                                      ALU.mult).then_inc(xn2_ready, 1)
                if prep:
                    dve.wait_ge(g_loaded[n.slot], n.turn * 16 + 16)
                    dve.scalar_tensor_tensor(gin[n.slot], xn[:, :], dis2[:, bass.ds(n.n, 1)], gin[n.slot],
                                             ALU.mult, ALU.add).then_inc(y_ready, 1)
                if (t - 2).within(NT):
                    for h in range(2):
                        o = xp[(t - 2).slot][:, h * HALF:(h + 1) * HALF]
                        dve.wait_ge(ffn_done, count_of(t - 2, 2, h + 1))
                        dve.tensor_tensor(o, bank(6 + h), o, ALU.add).then_inc(out_ready, 1)
                if post:
                    low(p, n_hi, n_lo, fT_hi, fT_lo)
                if prep:
                    for h in range(2):
                        cols = slice(h * HALF, (h + 1) * HALF)
                        dve.wait_ge(qexp_done, count_of(n, 2, h + 1))
                        dve.scalar_tensor_tensor(phi[:, cols], bank(2 + h), 0.0, phi[:, cols], ALU.max, ALU.add)\
                           .then_inc(phiq_ready, 1)
                    low(n, y_hi, y_lo, yT_hi[n.slot], yT_lo[n.slot], s_y)
                if now:
                    mixed(t, 0)
                if post:
                    gate_in(p)
                if prep:
                    dve.wait_ge(phik_scaled, count_of(n, 2, 2))
                    dve.tensor_reduce(z16[:, :], phi[:, :].rearrange("p (h d) -> p h d", d=DH), AX_X, ALU.add)\
                       .then_inc(z_chain, 1)
                    dve.wait_ge(z_chain, count_of(n, 3, 1))
                    dve.tensor_scalar(z16[:, :], z16[:, :], Z_EPS, None, ALU.add).then_inc(z_chain, 1)
                    dve.wait_ge(z_chain, count_of(n, 3, 2))
                    dve.reciprocal(z16[:, :], z16[:, :]).then_inc(z_chain, 1)
                if post:
                    gate_out(p)
                if prep:
                    low(n, a_hi, a_lo, aT_hi[n.slot], aT_lo[n.slot], s_a)

            walk2(dve, step)


_INS = ['x', 'src', 'dst', 'L0_gnn_W', 'L0_gnn_b', 'L0_mix_Wq', 'L0_mix_Wk', 'L0_mix_Wv', 'L0_mix_Wo',
        'L0_ffn_w_in', 'L0_ffn_w_out', 'L0_ffn_w1', 'L0_ffn_w2', 'L0_ffn_wg', 'L0_ffn_we', 'L0_ffn_gb', 'L0_ffn_eb']


def kernel(**inputs):
    import numpy as _np
    import concourse.bacc as _bacc
    from concourse import mybir as _mybir
    from concourse.bass_utils import run_bass_kernel_spmd as _run

    nc = _bacc.Bacc("TRN2", target_bir_lowering=False, num_devices=1)
    arrays, args = {}, []
    for name in _INS:
        a = _np.ascontiguousarray(inputs[name])
        arrays[f"in_{name}_dram"] = a
        args.append(nc.dram_tensor(f"in_{name}_dram", a.shape, _mybir.dt.from_np(a.dtype), kind="ExternalInput").ap())
    shape = inputs["x"].shape
    args.append(nc.dram_tensor("out_0_dram", shape, _mybir.dt.float32, kind="ExternalOutput").ap())
    gps_layer(nc, *args)
    r = _run(nc, [arrays], core_ids=[0])
    return r.results[0]["out_0_dram"]
```

```python
from contextlib import ExitStack

import concourse.bass as bass
from concourse import mybir

ALU = mybir.AluOpType
ACT = mybir.ActivationFunctionType
AX_X = mybir.AxisListType.X
F32 = mybir.dt.float32
F32R = mybir.dt.float32r
F16 = mybir.dt.float16
I32 = mybir.dt.int32
U32 = mybir.dt.uint32

P = 128
RING = 3
HALF = 512
LN_EPS = 1e-5
LN_SCALE = 1024.0
Z_EPS = 1e-6
Y_SCALE_MAX = 32.0
A_SCALE_MAX = float(2 ** 14)
W_TOP = float(2 ** 15)
BIG = 1e30


class Tile:

    def __init__(self, base, i=None):
        self.base, self.i = base, i
        self.slot = base % RING
        self.n = base if i is None else i * RING + base
        self.turn = base // RING if i is None else i + base // RING

    def __add__(self, d):
        return Tile(self.base + d, self.i)

    def __sub__(self, d):
        return Tile(self.base - d, self.i)

    def within(self, count):
        return self.i is not None or 0 <= self.base < count


def count_of(tile, per, k):
    return tile.n * per + k


def carry(eng, cell):
    return eng.tensor_tensor(cell[0:1, 1:2], cell[0:1, 0:1], cell[0:1, 0:1], ALU.add)


def wait(eng, sem, value):
    if not isinstance(value, int) or value > 0:
        eng.wait_ge(sem, value)


def gps_layer(nc, x, src, dst, gnn_W, gnn_b, Wq, Wk, Wv, Wo, w_in, w_out, w1, w2, wg, we, gb, eb, out):
    N, D = x.shape
    E = src.shape[0]
    H, DH = Wq.shape[0], Wq.shape[1]
    HID = w_out.shape[1]
    NEXP = w2.shape[0]
    NGRP = wg.shape[0]
    EPG = NEXP // NGRP
    C = D // P
    CH = C // 2
    NTF, REM = N // P, N % P
    NT = NTF + 1
    EP = 125
    ET = E // EP
    FIN = 4 * HID + NGRP + NEXP
    assert D == 1024 and DH == 64 and H * DH == D and REM and E == EP * ET and EPG * NGRP == NEXP
    assert NGRP == 2 and HID == 32 and NEXP == 8
    G_ROWS = (NT + 1) * P
    PAD_SRC = N

    P1_FIRST = 4
    P1_A = (NT - P1_FIRST - RING * ET - 4) // RING
    assert P1_A >= 1
    P2_FIRST = 2
    P2_TURNS = (NTF - 2 - P2_FIRST) // RING

    agg = nc.dram_tensor("agg_rows", (G_ROWS, D), F32, kind="Internal").ap()
    P1_BEFORE = P1_FIRST + RING * P1_A
    P1_LAST = P1_BEFORE + RING * ET
    WO_LOADS = 3
    assert NT > P1_LAST + WO_LOADS
    P1_ZERO = P1_BEFORE + RING
    ZSTEP = min(2, (NT + 1) // P1_ZERO)
    ZPREP = NT + 1 - ZSTEP * P1_ZERO
    ZCUTS = sorted({0, ZPREP, *range(8, ZPREP, 4)})
    ZPARTS = len(ZCUTS) - 1 + P1_ZERO

    with ExitStack() as ctx:
        def sb(name, shape, dt=F32):
            return ctx.enter_context(nc.sbuf_tensor(name, shape, dt))

        def sem(name):
            return ctx.enter_context(nc.semaphore(name))

        w2_hi = sb("w2_hi", [P, NGRP, D], F32R)
        w2_lo = sb("w2_lo", [P, NGRP, D], F32R)
        wo3 = sb("wo3", [3 * HID, D], F32R)
        hwT_hi = sb("hwT_hi", [P, NGRP, P], F32R)
        hwT_lo = sb("hwT_lo", [P, NGRP, P], F32R)
        sh3T = sb("sh3T", [3 * HID, P], F32R)
        w_hi = sb("w_hi", [P, C, D], F16)
        w_lo = sb("w_lo", [P, C, D], F16)
        xT_hi = sb("xT_hi", [P, C, P], F16)
        xT_lo = sb("xT_lo", [P, C, P], F16)
        nT_hi = sb("nT_hi", [P, C, P], F16)
        nT_lo = sb("nT_lo", [P, C, P], F16)
        wq_hi = sb("wq_hi", [P, C, P], F16)
        wq_lo = sb("wq_lo", [P, C, P], F16)
        fin_hi = sb("fin_hi", [P, C, FIN], F16)
        fin_lo = sb("fin_lo", [P, C, FIN], F16)
        mreg = sb("mreg", [P, C * D])
        m_hi = mreg[:, 0:C * D // 2].bitcast(F16).rearrange("p (c n) -> p c n", c=C)
        m_lo = mreg[:, C * D // 2:].bitcast(F16).rearrange("p (c n) -> p c n", c=C)
        XNW = C * (P + 1)
        phi1 = [mreg[:, s * D:(s + 1) * D] for s in range(RING)]
        xn1 = [mreg[:, 3 * D + s * XNW:3 * D + (s + 1) * XNW].rearrange("p (c f) -> p c f", c=C)
               for s in range(RING)]
        ex1 = mreg[:, 3 * D + 3 * XNW:4 * D + 3 * XNW]
        ohb = mreg[:, 0:ET * P].rearrange("p (t b) -> p t b", b=P)
        oha = mreg[:, ET * P:ET * (P + NT)].rearrange("p (t b) -> p t b", b=NT)
        ohn = mreg[:, ET * (P + NT):ET * (P + 2 * NT)].rearrange("p (t b) -> p t b", b=NT)
        oha_dst = ohn
        w2rows = mreg[:, 5 * D + 768:7 * D + 768].rearrange("p (n e h) -> p n e h", n=C, e=NEXP)
        assert ET * (P + 2 * NT) <= 5 * D + 768
        zreg = sb("zreg", [P, 9 * D])
        wrows = zreg[:, 0:8 * D].rearrange("p (o i) -> p o i", o=C)
        worows = wrows
        zeros = zreg[:, 8 * D:9 * D]
        parts = zreg[:, 0:6 * D].bitcast(F16).rearrange("p (s k c n) -> p s k c n", s=RING, k=4, c=C)
        yT_hi, yT_lo, aT_hi, aT_lo = [[parts[:, s, k] for s in range(RING)] for k in range(4)]
        xp = [zreg[:, (6 + s) * D:(7 + s) * D] for s in range(RING)]
        xreg = sb("xreg", [P, 3 * D])
        xin = [xreg[:, s * D:(s + 1) * D] for s in range(RING)]
        ohb_dst = xreg[:, 0:ET * P].rearrange("p (t b) -> p t b", b=P)
        greg = sb("greg", [P, 3 * D])
        gin = [greg[:, s * D:(s + 1) * D] for s in range(RING)]
        srcb = greg[:, 0:P * ET].bitcast(I32).rearrange("p (e t) -> p e t", t=ET)
        dgm = gin[2].rearrange("p (c n) -> p c n", c=C)
        xn = sb("xn", [P, D])
        xe = xn
        wcat1 = xn
        xn2 = sb("xn2", [P, D])
        msum = xn2
        wcat2 = xn2[0:NGRP + NEXP, :]
        phi = sb("phi", [P, D])
        x1T = phi[:, :].rearrange("p (c n) -> p c n", c=C)
        wout3 = phi[:, 0:3 * HID * C].rearrange("p (n k) -> p n k", n=C)
        ksb = sb("ksb", [P, D])
        wqbd = ksb[:, :].rearrange("p (c n) -> p c n", c=C)
        wkb = sb("wkb", [P, D])
        wkbd = wkb[:, :].rearrange("p (c n) -> p c n", c=C)
        bias_b = wkb
        wvbd = sb("wvbd", [P, C, P])
        kvn = xn[:, :].rearrange("p (c n) -> p c n", c=C)
        kvnT = xn2[:, :].rearrange("p (c n) -> p c n", c=C)
        kvT = phi[:, :].rearrange("p (c n) -> p c n", c=C)

        pool_cell = sb("pool_cell", [1, 2])
        dve_cell = sb("dve_cell", [1, 2])
        ident = sb("ident", [P, P])
        ones = sb("ones", [P, P])
        below = sb("below", [P, P])
        bdmask = sb("bdmask", [P, P])
        same = sb("same", [P, P])
        same_t = sb("same_t", [P, P])
        iota_i = sb("iota_i", [P, P], I32)
        iota_f = sb("iota_f", [P, P])
        dump_f = sb("dump_f", [P, 1])
        dump_i = sb("dump_i", [P, 1], I32)
        ohT = sb("ohT", [NT, 2, HALF])
        src_i = sb("src_i", [P, ET], I32)
        dst_i = sb("dst_i", [P, ET], I32)
        src_f = sb("src_f", [P, ET])
        ab_i = sb("ab_i", [P, 2, ET], I32)
        ab_f = sb("ab_f", [P, 2, ET])
        dis = sb("dis", [P, NT])
        disT = sb("disT", [NT, P])
        dis_src = sb("dis_src", [P, ET])
        dis_dst = sb("dis_dst", [P, ET])
        norm = sb("norm", [P, ET])
        rowsum = sb("rowsum", [P, NT])
        dis2 = sb("dis2", [P, NT])
        mhalf = sb("mhalf", [P, NT])
        stats = sb("stats", [P, 2, 6])
        mv = [sb(f"mv_slot{s}", [P, 2]) for s in range(RING)]
        mvt = sb("mvt", [P, NT, 2])
        e_dst = sb("e_dst", [P, 1], I32)
        e_idx = sb("e_idx", [P, 1], I32)
        e_sc = sb("e_sc", [P, 8])
        e_stats = sb("e_stats", [P, 2, 6])
        e_mv = sb("e_mv", [P, 2])
        NMAX = 4
        ks = sb("ks", [P, C])
        rk = sb("rk", [P, C])
        mx = sb("mx", [P, NMAX])
        mxo = sb("mxo", [P, C])
        row = sb("row", [1, 4])
        sc = sb("sc", [P, 14])
        (s_w, s_q, s_f, s_m, s_t, s_y, s_a, t_inv, q_inv, f_inv, q_ninv, f_ninv, tmp0, tmp1) = [
            sc[:, k:k + 1] for k in range(14)]
        z16 = sb("z16", [P, H])
        stats2 = sb("stats2", [P, 2, 6])
        mv2 = sb("mv2", [P, 2])
        gbias = sb("gbias", [P, NGRP + NEXP])
        pen_a = sb("pen_a", [P, NEXP])
        pen_b = sb("pen_b", [P, NEXP])
        tri = sb("tri", [P, NEXP, NEXP])
        lg = sb("lg", [P, NGRP + NEXP])
        gs = sb("gs", [P, 8])
        v8 = sb("v8", [P, NEXP])
        NSIL = 2 * HID
        exb = sb("exb", [P, 1 + NSIL + NEXP])
        rec = sb("rec", [P, 1 + NSIL])
        hs = sb("hs", [P, NSIL])
        gt = sb("gt", [P, NEXP, NEXP])
        eq = sb("eq", [P, NEXP, NEXP])
        rank = sb("rank", [P, NEXP])
        hw = sb("hw", [P, NEXP, HID])
        sh3 = sb("sh3", [P, 3 * HID], F32R)

        ps = ctx.enter_context(nc.psum_tensor("ps", [P, 8, HALF], F32))

        def bank(b):
            return ps[:, b, :]

        idx_loaded = sem("idx_loaded")
        srcb_loaded = sem("srcb_loaded")
        w_loaded = sem("w_loaded")
        wq_loaded = sem("wq_loaded")
        bd_loaded = sem("bd_loaded")
        cat_loaded = sem("cat_loaded")
        ffn_loaded = sem("ffn_loaded")
        wo_loaded = sem("wo_loaded")
        bias_loaded = sem("bias_loaded")
        consts = sem("consts")
        consts_dve = sem("consts_dve")
        prep_dve = sem("prep_dve")
        prep_pe = sem("prep_pe")
        prep_pool = sem("prep_pool")
        oh_turned = sem("oh_turned")
        ohT_ready = sem("ohT_ready")
        dis_picked = sem("dis_picked")
        job_done = sem("job_done")
        job_hi = sem("job_hi")
        job_lo = sem("job_lo")
        wq_split = sem("wq_split")
        agg_zeroed = sem("agg_zeroed")
        agg_added = sem("agg_added")
        x1_loaded = [sem(f"x1_loaded{s}") for s in range(RING)]
        stats1_done = sem("stats1_done")
        var1_ready = sem("var1_ready")
        rstd1_ready = sem("rstd1_ready")
        mv_kept = sem("mv_kept")
        xn1_ready = sem("xn1_ready")
        x1_turned = sem("x1_turned")
        x1T_ready = sem("x1T_ready")
        k_done = sem("k_done")
        kexp_done = sem("kexp_done")
        k_neg = sem("k_neg")
        phik_ready = sem("phik_ready")
        kv_done = sem("kv_done")
        e_cols = sem("e_cols")
        e_chain = sem("e_chain")
        e_gathered = sem("e_gathered")
        e_rstd = sem("e_rstd")
        e_summed = sem("e_summed")
        e_out_dve = sem("e_out_dve")
        e_out_act = sem("e_out_act")
        e_carried = sem("e_carried")
        mid_dve = sem("mid_dve")
        mid_pe = sem("mid_pe")
        mid_act = sem("mid_act")
        m_done = sem("m_done")
        m_hi_done = sem("m_hi_done")
        m_lo_done = sem("m_lo_done")
        x2_loaded = [sem(f"x2_loaded{s}") for s in range(RING)]
        g_loaded = [sem(f"g_loaded{s}") for s in range(RING)]
        stored = [sem(f"stored{s}") for s in range(RING)]
        xn_ready = sem("xn_ready")
        y_ready = sem("y_ready")
        a_ready = sem("a_ready")
        xn2_ready = sem("xn2_ready")
        x_turned, x_hi, x_lo = sem("x_turned"), sem("x_hi"), sem("x_lo")
        y_turned, y_hi, y_lo = sem("y_turned"), sem("y_hi"), sem("y_lo")
        a_turned, a_hi, a_lo = sem("a_turned"), sem("a_hi"), sem("a_lo")
        n_turned, n_hi, n_lo = sem("n_turned"), sem("n_hi"), sem("n_lo")
        h_turned, h_hi, h_lo = sem("h_turned"), sem("h_hi"), sem("h_lo")
        q_done = sem("q_done")
        q_chain = sem("q_chain")
        qexp_done = sem("qexp_done")
        elu_ready = sem("elu_ready")
        z_chain = sem("z_chain")
        mix_done = sem("mix_done")
        mix_read = sem("mix_read")
        xp_ready = sem("xp_ready")
        ln2_chain = sem("ln2_chain")
        rstd2_ready = sem("rstd2_ready")
        fin_done = sem("fin_done")
        gate_chain = sem("gate_chain")
        gate_exp = sem("gate_exp")
        ffn_done = sem("ffn_done")
        out_ready = sem("out_ready")

        block = ctx.enter_context(nc.Block())

        def rows_of(t):
            if t.i is None and t.base == NTF:
                return slice(NTF * P, N), REM
            return (bass.ds(t.n * P, P) if t.i is not None else slice(t.base * P, (t.base + 1) * P)), P

        def walk1(eng, step, edge):
            for t in range(P1_FIRST):
                step(Tile(t))
            with eng.Fori(0, P1_A) as i:
                for u in range(RING):
                    step(Tile(P1_FIRST + u, i))
            first = P1_FIRST + RING * P1_A
            for u in range(RING):
                if u > 0:
                    edge(0, u)
                step(Tile(first + u))
            edge(0, RING)
            with eng.Fori(1, ET) as i:
                for u in range(RING):
                    edge(i, u)
                    step(Tile(first + u, i))
                edge(i, RING)
            for t in range(first + RING * ET, NT):
                step(Tile(t))

        def walk2(eng, step):
            for t in range(-1, P2_FIRST):
                step(Tile(t))
            with eng.Fori(0, P2_TURNS) as i:
                for u in range(RING):
                    step(Tile(P2_FIRST + u, i))
            for t in range(P2_FIRST + RING * P2_TURNS, NT + 2):
                step(Tile(t))

        JOBS = ([("w", c, h) for c in range(C) for h in range(2)] + [("fin", c, 0) for c in range(C)]
                + [("wo", 0, h) for h in range(2)] + [("w2", g, h) for g in range(NGRP) for h in range(2)])
        GROUPS = [(end, k, min(k + 4, ET)) for end in ("dst", "src") for k in range(0, ET, 4)]
        assert len(GROUPS) < 2 * C
        NCONST = 10
        BD = 2
        PREP_HOT, PREP_HOT_DST, PREP_DEG, PREP_MAX, PREP_POW, PREP_SCALE, PREP_DIST = 8, 13, 14, 18, 24, 25, 29
        PREP_OHN = PREP_DIST + 2 * len(GROUPS) + 3
        PREP_ALL = PREP_OHN + 4
        MID_KVN, MID_MAX, MID_ROW, MID_SCALE, MID_ALL = C + 13, C + 23, C + 30, C + 31, C + 39
        GATE_EXP, GATE_N = 9, 27

        @block.sync
        def _(sp):
            sp.wait_ge(consts, NCONST)
            sp.dma_start(src_i[0:EP, :], src.rearrange("(p t) -> p t", t=ET)).then_inc(idx_loaded, 16)
            sp.dma_start(dst_i[0:EP, :], dst.rearrange("(p t) -> p t", t=ET)).then_inc(idx_loaded, 16)

            def load_blocks(w, t, loaded):
                two = w.rearrange("(c i) d e -> i d c e", i=2)
                for k in range(2):
                    sp.dma_start(t[k * DH:(k + 1) * DH, :, k * DH:(k + 1) * DH], two[k]).then_inc(loaded, 16)

            load_blocks(Wq, wqbd, wq_loaded)
            sp.dma_start(wcat1[0:2 * HID, :], w_in).then_inc(cat_loaded, 16)
            sp.dma_start(wcat1[2 * HID:4 * HID, :], w1).then_inc(cat_loaded, 16)
            sp.dma_start(wcat2[0:NGRP, :], wg).then_inc(cat_loaded, 16)
            sp.dma_start(wcat2[NGRP:, :], we).then_inc(cat_loaded, 16)
            sp.dma_start(wrows, gnn_W.rearrange("(o p) i -> p o i", p=P)).then_inc(w_loaded, 16)
            load_blocks(Wk, wkbd, bd_loaded)
            load_blocks(Wv, wvbd[:, :, :], bd_loaded)

            def load1(t):
                r, n = rows_of(t)
                sp.dma_start(xin[t.slot][0:n, :], x[r, :]).then_inc(x1_loaded[t.slot], 16)

            for k in range(3):
                sp.dma_start(wout3[:, :, k * HID:(k + 1) * HID],
                             w_out.rearrange("(n p) h -> p n h", p=P)).then_inc(ffn_loaded, 16)
            for e in range(NEXP):
                sp.dma_start(w2rows[:, :, e, :], w2[e].rearrange("(n p) h -> p n h", p=P)).then_inc(ffn_loaded, 16)
            sp.dma_start(gbias[:, 0:NGRP], gb.partition_broadcast(P)).then_inc(ffn_loaded, 16)
            sp.dma_start(gbias[:, NGRP:], eb.partition_broadcast(P)).then_inc(ffn_loaded, 16)
            sp.dma_start(srcb[:, 0:EP, :], src.rearrange("(p t) -> p t", t=ET).partition_broadcast(P))\
              .then_inc(srcb_loaded, 16)
            sp.wait_ge(prep_dve, PREP_OHN)
            for t in range(RING):
                load1(Tile(t))

            def step(t):
                if (t + RING).within(NT):
                    sp.wait_ge(xn1_ready, count_of(t, 1, 1))
                    load1(t + RING)
                if t.i is None and 0 <= t.base - P1_LAST < WO_LOADS:
                    k = t.base - P1_LAST
                    c = slice(k * C // WO_LOADS, (k + 1) * C // WO_LOADS)
                    sp.wait_ge(job_done, 2 * C)
                    sp.wait_ge(xn1_ready, t.base + 1)
                    sp.dma_start(worows[:, c, :], Wo.rearrange("(c p) n -> p c n", p=P)[:, c, :])\
                      .then_inc(wo_loaded, 16)

            def edge(i, part):
                pass

            walk1(sp, step, edge)

            sp.wait_ge(k_done, 2 * NT)
            sp.dma_start(bias_b[:, :], gnn_b.partition_broadcast(P)).then_inc(bias_loaded, 16)

            def load2(t):
                r, n = rows_of(t)
                sp.dma_start(xin[t.slot][0:n, :], x[r, :]).then_inc(x2_loaded[t.slot], 16)
                sp.dma_start(gin[t.slot][0:n, :], agg[r, :]).then_inc(g_loaded[t.slot], 16)

            sp.wait_ge(xn1_ready, NT)
            sp.wait_ge(agg_zeroed, 16 * ZPARTS)
            sp.wait_ge(agg_added, 16 * ET)
            load2(Tile(0))

            def step(t):
                if (t + 2).within(NT):
                    wait(sp, xp_ready, count_of(t - 1, 2, 2))
                    wait(sp, y_turned, count_of(t - 1, 2, 2))
                    if t.base == 0:
                        sp.wait_ge(mid_pe, 5)
                    load2(t + 2)
                if (t - 2).within(NT):
                    sp.wait_ge(out_ready, count_of(t - 2, 2, 2))
                    r, n = rows_of(t - 2)
                    sp.dma_start(out[r, :], xp[(t - 2).slot][0:n, :]).then_inc(stored[(t - 2).slot], 16)

            walk2(sp, step)
            for s in range(RING):
                sp.wait_ge(stored[s], 16 * len(range(s, NT, RING)))

        @block.gpsimd
        def _(pool):
            pool.memset(src_i[:, :], PAD_SRC).then_inc(consts, 1)
            pool.memset(dst_i[:, :], 0).then_inc(consts, 1)
            pool.memset(srcb, PAD_SRC).then_inc(consts, 1)
            pool.memset(wqbd, 0.0).then_inc(consts, 1)
            pool.memset(wkbd, 0.0).then_inc(consts, 1)
            pool.memset(wvbd[:, :, :], 0.0).then_inc(consts, 1)
            pool.memset(ident[:, :], 0.0).then_inc(consts, 1)
            pool.memset(below[:, :], 1.0).then_inc(consts, 1)
            pool.memset(tri[:, :, :], 1.0).then_inc(consts, 1)
            pool.memset(pool_cell[:, :], 0.0).then_inc(consts, 1)
            pool.wait_ge(consts, NCONST)
            pool.affine_select(out=ident[:, :], in_=ident[:, :], compare_op=ALU.not_equal, fill=1.0, base=0,
                               pattern=[[-1, P]], channel_multiplier=1).then_inc(prep_pool, 1)
            pool.iota(iota_i[:, :], pattern=[[1, P]], base=0, channel_multiplier=0).then_inc(prep_pool, 1)
            pool.iota(dump_i[:, :], pattern=[[0, 1]], base=NT * P, channel_multiplier=1).then_inc(prep_pool, 1)
            pool.affine_select(out=below[:, :], in_=below[:, :], compare_op=ALU.is_gt, fill=0.0, base=0,
                               pattern=[[-1, P]], channel_multiplier=1).then_inc(prep_pool, 1)
            pool.affine_select(out=tri[:, :, :], in_=tri[:, :, :], compare_op=ALU.is_gt, fill=0.0, base=0,
                               pattern=[[1, NEXP], [-1, NEXP]], channel_multiplier=0).then_inc(prep_pool, 1)
            pool.memset(mhalf[:, :], -0.5).then_inc(prep_pool, 1)
            pool.wait_ge(prep_dve, PREP_DEG)
            pool.wait_ge(prep_pool, 6)
            pool.tensor_tensor(dis[:, :], dis[:, :], mhalf[:, :], ALU.pow).then_inc(prep_pool, 1)

            def rstd1(t):
                pool.wait_ge(var1_ready, count_of(t, 2, 2))
                m = mv[t.slot]
                pool.tensor_tensor(m[:, 1:2], m[:, 1:2], mhalf[:, 0:1], ALU.pow).then_inc(rstd1_ready, 1)
                pool.wait_ge(rstd1_ready, count_of(t, 2, 1))
                pool.tensor_tensor(m[:, 0:1], m[:, 0:1], m[:, 1:2], ALU.mult).then_inc(rstd1_ready, 1)
                pool.wait_ge(rstd1_ready, count_of(t, 2, 2))
                pool.tensor_copy(mvt[:, bass.ds(t.n, 1), :], m[:, None, :]).then_inc(mv_kept, 1)

            rstd1(Tile(0))
            rstd1(Tile(1))
            pool.wait_ge(job_done, len(JOBS))

            def step(t):
                if (t + 2).within(NT):
                    rstd1(t + 2)

            def edge(i, part):
                if part == 0:
                    pool.wait_ge(e_cols, i * 3 + 1)
                    wait(pool, e_summed, i * 2)
                    wait(pool, e_carried, i * 2 - 1)
                    carry(pool, pool_cell).then_inc(e_carried, 1)
                    pool.indirect_dma_start(
                        out=xe[:, :], out_offset=None, in_=x,
                        in_offset=bass.IndirectOffsetOnAxis(ap=e_dst[:, :].bitcast(U32), axis=0),
                    ).then_inc(e_gathered, 16)
                if part == 1:
                    pool.wait_ge(e_chain, i * 11 + 8)
                    pool.tensor_tensor(e_mv[:, 1:2], e_mv[:, 1:2], mhalf[:, 0:1], ALU.pow).then_inc(e_rstd, 1)
                    if not isinstance(i, int) or i > 0:
                        scatter(i, i * 2)

            def scatter(n, carried):
                pool.wait_ge(e_out_dve, n)
                pool.wait_ge(e_out_act, n)
                pool.wait_ge(e_chain, n * 11)
                pool.wait_ge(agg_zeroed, 16 * ZPARTS)
                pool.wait_ge(e_carried, carried)
                carry(pool, pool_cell).then_inc(e_carried, 1)
                pool.indirect_dma_start(
                    out=agg, out_offset=bass.IndirectOffsetOnAxis(ap=e_idx[:, :].bitcast(U32), axis=0),
                    in_=msum[:, :], in_offset=None, compute_op=ALU.add,
                ).then_inc(agg_added, 16)

            edge(0, 0)
            walk1(pool, step, edge)
            scatter(ET, ET * 2 - 1)

            def step(t):
                if (t - 1).within(NT):
                    pool.wait_ge(ln2_chain, count_of(t - 1, 3, 3))
                    pool.tensor_tensor(mv2[:, 1:2], mv2[:, 1:2], mhalf[:, 0:1], ALU.pow).then_inc(rstd2_ready, 1)
                if (t + 1).within(NT):
                    n = t + 1
                    pool.wait_ge(z_chain, count_of(n, 4, 4))
                    p3 = phi[:, :].rearrange("p (h d) -> p h d", d=DH)
                    pool.tensor_tensor(p3, p3, z16[:, :, None].to_broadcast([P, H, DH]), ALU.mult)\
                        .then_inc(a_ready, 1)

            walk2(pool, step)

        @block.scalar
        def _(act):
            act.wait_ge(consts_dve, 1)
            act.wait_ge(w_loaded, 16)

            def zero(k):
                a, b = ZCUTS[k], ZCUTS[k + 1]
                act.dma_start(agg[a * P:b * P, :].rearrange("(p a) d -> p a d", p=P),
                              zeros[:, None, :].to_broadcast([P, b - a, D])).then_inc(agg_zeroed, 16)

            def pick(g):
                n = (GROUPS[g][2] - GROUPS[g][1]) * P
                act.wait_ge(oh_turned, g + 1)
                wait(act, dis_picked, g - 1)
                act.activation(ohT[:, g % 2, 0:n], bank(4 + g % 2)[0:NT, 0:n], ACT.Copy).then_inc(ohT_ready, 1)

            zero(0)
            act.wait_ge(prep_dve, PREP_SCALE)
            pick(0)
            for j, (kind, c, h) in enumerate(JOBS):
                if j % 2 == 0 and j // 2 + 2 < len(ZCUTS):
                    zero(j // 2 + 1)
                if j + 1 < len(GROUPS):
                    pick(j + 1)
                act.wait_ge(job_done, j + 1)
                b = bank(j % 2)
                if kind == "w":
                    o = act.activation(w_hi[:, c, h * HALF:(h + 1) * HALF], b, ACT.Copy, scale=s_w)
                elif kind == "fin":
                    o = act.activation(fin_hi[:, c, :], b[:, 0:FIN], ACT.Copy, scale=s_f)
                elif kind == "wo":
                    o = act.activation(wo3[:, h * HALF:(h + 1) * HALF], b[0:3 * HID, :], ACT.Copy)
                else:
                    o = act.activation(w2_hi[:, c, h * HALF:(h + 1) * HALF], b, ACT.Copy)
                o.then_inc(job_hi, 1)

            def negative_exp(o, i, negated, done, count):
                act.activation(o, i, ACT.Relu, scale=-1.0).then_inc(negated, 1)
                act.wait_ge(negated, count)
                act.activation(o, o, ACT.Exp, scale=-1.0).then_inc(done, 1)

            def normal(t):
                act.wait_ge(rstd1_ready, count_of(t, 2, 2))
                wait(act, kv_done, count_of(t - RING, 1, 1))
                m = mv[t.slot]
                act.activation(xn1[t.slot][:, :, 0:P], xin[t.slot][:, :].rearrange("p (c f) -> p c f", c=C),
                               ACT.Identity, bias=m[:, 0:1], scale=m[:, 1:2]).then_inc(xn1_ready, 1)

            def turn(t):
                for h in range(2):
                    act.wait_ge(x1_turned, count_of(t, 2, h + 1))
                    wait(act, k_done, count_of(t - 1, 2, h + 1))
                    act.activation(x1T[:, h * CH:(h + 1) * CH, :].rearrange("p c n -> p (c n)"), bank(h),
                                   ACT.Copy).then_inc(x1T_ready, 1)

            act.wait_ge(prep_dve, PREP_ALL)
            normal(Tile(0))
            turn(Tile(0))

            def step(t):
                if (t + 1).within(NT):
                    normal(t + 1)
                for h in range(2):
                    act.wait_ge(k_done, count_of(t, 2, h + 1))
                    wait(act, phik_ready, count_of(t - 1, 2, h + 1))
                    negative_exp(ex1[:, h * HALF:(h + 1) * HALF], bank(2 + h), k_neg, kexp_done, count_of(t, 2, h + 1))
                if (t + 1).within(NT):
                    turn(t + 1)
                if t.base < (P1_ZERO if t.i is None else P1_BEFORE):
                    act.dma_start(agg[bass.ds((t.n * ZSTEP + ZPREP) * P, ZSTEP * P), :]
                                  .rearrange("(p a) d -> p a d", p=P),
                                  zeros[:, None, :].to_broadcast([P, ZSTEP, D])).then_inc(agg_zeroed, 16)

            def edge(i, part):
                if part == RING:
                    wait(act, agg_added, i * 16)
                    act.wait_ge(e_summed, i * 2 + 2)
                    act.activation(msum[:, HALF:D], bank(7), ACT.Copy).then_inc(e_out_act, 1)

            walk1(act, step, edge)

            act.wait_ge(mid_pe, 1)
            act.wait_ge(agg_added, 16 * ET)
            for h in range(2):
                act.activation(kvnT[:, h * CH:(h + 1) * CH, :].rearrange("p c n -> p (c n)"), bank(h),
                               ACT.Copy).then_inc(mid_act, 1)
            act.wait_ge(mid_pe, 2)
            for h in range(2):
                act.activation(kvT[:, h * CH:(h + 1) * CH, :].rearrange("p c n -> p (c n)"), bank(2 + h),
                               ACT.Copy).then_inc(mid_act, 1)
            act.wait_ge(mid_pe, 5)
            for h in range(2):
                act.activation(ksb[:, h * HALF:(h + 1) * HALF], bank(h), ACT.Copy).then_inc(mid_act, 1)
            act.wait_ge(mid_dve, MID_SCALE)
            for j in range(2 * C):
                act.wait_ge(m_done, j + 1)
                act.activation(m_hi[:, j // 2, (j % 2) * HALF:(j % 2 + 1) * HALF], bank(4 + j % 4), ACT.Copy,
                               scale=s_m).then_inc(m_hi_done, 1)

            def normalise(t):
                act.wait_ge(x2_loaded[t.slot], t.turn * 16 + 16)
                wait(act, x_turned, count_of(t - 1, 2, 2))
                wait(act, y_ready, count_of(t - 1, 1, 1))
                act.activation(xn[:, :], xin[t.slot][:, :], ACT.Identity, bias=mvt[:, bass.ds(t.n, 1), 0:1].rearrange("p a b -> p (a b)"),
                               scale=mvt[:, bass.ds(t.n, 1), 1:2].rearrange("p a b -> p (a b)"))\
                   .then_inc(xn_ready, 1)

            def high(t, turned, done, dest, scale=1.0):
                for h in range(2):
                    act.wait_ge(turned, count_of(t, 2, h + 1))
                    act.activation(dest[:, h * CH:(h + 1) * CH, :].rearrange("p c n -> p (c n)"), bank(h),
                                   ACT.Copy, scale=scale).then_inc(done, 1)

            act.wait_ge(mid_pe, 3)
            act.wait_ge(mid_dve, MID_ALL)
            act.wait_ge(mv_kept, NT)
            normalise(Tile(0))

            def step(t):
                if (t - 2).within(NT):
                    act.wait_ge(h_turned, count_of(t - 2, 1, 1))
                    wait(act, ffn_done, count_of(t - 3, 2, 2))
                    act.activation(hwT_hi[:, :, :].rearrange("p c n -> p (c n)"), ps[:, 7, 0:2 * P], ACT.Copy)\
                       .then_inc(h_hi, 1)
                    act.activation(sh3T[:, :], ps[0:3 * HID, 7, 2 * P:3 * P], ACT.Copy).then_inc(h_hi, 1)
                if (t + 1).within(NT):
                    n = t + 1
                    wait(act, q_done, count_of(t, 2, 2))
                    high(n, x_turned, x_hi, xT_hi, LN_SCALE)
                    wait(act, a_turned, count_of(t, 2, 2))
                    for h in range(2):
                        act.wait_ge(q_done, count_of(n, 2, h + 1))
                        e = phi[:, h * HALF:(h + 1) * HALF]
                        act.activation(e, bank(2 + h), ACT.Relu, scale=q_ninv).then_inc(q_chain, 1)
                        act.wait_ge(q_chain, count_of(n, 4, 2 * h + 1))
                        act.activation(e, e, ACT.Exp, scale=-1.0).then_inc(q_chain, 1)
                        act.wait_ge(q_chain, count_of(n, 4, 2 * h + 2))
                        act.activation(e, e, ACT.Copy, bias=-1.0).then_inc(qexp_done, 1)
                if (t - 1).within(NT):
                    wait(act, fin_done, count_of(t - 2, 1, 1))
                    high(t - 1, n_turned, n_hi, nT_hi, LN_SCALE)
                if (t + 1).within(NT):
                    n = t + 1
                    wait(act, mix_done, count_of(t - 2, 2, 2))
                    high(n, y_turned, y_hi, yT_hi[n.slot], s_y)
                if (t - 1).within(NT):
                    p = t - 1
                    act.wait_ge(gate_chain, count_of(p, GATE_N, GATE_EXP))
                    act.activation(exb[:, :], exb[:, :], ACT.Exp).then_inc(gate_exp, 1)
                if (t + 1).within(NT):
                    high(t + 1, a_turned, a_hi, aT_hi[(t + 1).slot], s_a)
                if (t + 2).within(NT):
                    normalise(t + 2)

            walk2(act, step)

        @block.tensor
        def _(pe):
            def wide(b, per, c):
                return bank(b)[:, c * per:(c + 1) * per]

            pe.wait_ge(consts_dve, 3)
            pe.wait_ge(prep_pool, 1)
            pe.wait_ge(prep_dve, PREP_HOT)
            for k in range(ET):
                mm = pe.matmul(bank(2)[:, 0:NT], ohb[:, k, :], oha[:, k, :], start=(k == 0), stop=(k == ET - 1))
            mm.then_inc(prep_pe, 1)
            pe.wait_ge(prep_pool, 7)
            pe.matmul(bank(2)[0:NT, 0:P], dis[:, :], ident[:, :], start=True, stop=True).then_inc(prep_pe, 1)
            pe.wait_ge(prep_dve, PREP_MAX)
            for k in range(NMAX):
                mm = pe.matmul(bank(3)[0:1, k * P:(k + 1) * P], mx[:, k:k + 1], ident[:, :], start=True, stop=True)
            mm.then_inc(prep_pe, 1)
            pe.wait_ge(prep_dve, PREP_POW)
            pe.matmul(bank(3)[:, 0:3], ones[0:1, :], row[0:1, 0:3], start=True, stop=True).then_inc(prep_pe, 1)
            def pick(g):
                end, k0, k1 = GROUPS[g]
                if g == 0:
                    pe.wait_ge(prep_dve, PREP_HOT_DST)
                wait(pe, ohT_ready, g - 1)
                for k in range(k0, k1):
                    mm = pe.transpose(wide(4 + g % 2, P, k - k0)[0:NT, :],
                                      (oha if end == "src" else oha_dst)[:, k, :], ident[:, :])
                mm.then_inc(oh_turned, 1)

            def picked(g):
                _, k0, k1 = GROUPS[g]
                pe.wait_ge(ohT_ready, g + 1)
                if g == 0:
                    pe.wait_ge(prep_dve, PREP_DIST)
                if g >= 2:
                    pe.wait_ge(prep_dve, PREP_DIST + 2 * (g - 1))
                for k in range(k0, k1):
                    mm = pe.matmul(wide(6 + g % 2, P, k - k0), ohT[:, g % 2, (k - k0) * P:(k - k0 + 1) * P],
                                   disT[:, :], start=True, stop=True)
                mm.then_inc(dis_picked, 1)

            pe.wait_ge(w_loaded, 16)
            pick(0)
            for j, (kind, c, h) in enumerate(JOBS):
                if j + 1 < len(GROUPS):
                    pick(j + 1)
                if j < len(GROUPS):
                    picked(j)
                if j == len(GROUPS) + 2:
                    pe.wait_ge(prep_dve, PREP_OHN)
                for k in range(4 * (j - len(GROUPS) - 2), min(4 * (j - len(GROUPS) - 1), ET)):
                    if k >= 0:
                        mm = pe.matmul(bank(3)[:, 0:NT], ohb[:, k, :], ohn[:, k, :], start=(k == 0),
                                       stop=(k == ET - 1))
                        if k == ET - 1:
                            mm.then_inc(prep_pe, 1)
                if j >= 2:
                    pe.wait_ge(job_lo, j - 1)
                if j == 2 * C:
                    pe.wait_ge(cat_loaded, 16 * 4)
                    pe.wait_ge(ffn_loaded, 16 * (3 + NEXP + 2))
                if kind == "fin":
                    mm = pe.transpose(wide(j % 2, P, 0), wcat1[:, c * P:(c + 1) * P], ident[:, :])
                    mm = pe.matmul(bank(j % 2)[:, P:FIN], wcat2[:, c * P:(c + 1) * P],
                                   ident[0:NGRP + NEXP, 0:NGRP + NEXP], start=True, stop=True)
                else:
                    for k in range(4):
                        if kind == "w":
                            mm = pe.transpose(wide(j % 2, P, k), wrows[:, h * 4 + k, c * P:(c + 1) * P],
                                              ident[:, :])
                        elif kind == "wo":
                            mm = pe.matmul(bank(j % 2)[0:3 * HID, k * P:(k + 1) * P], wout3[:, h * 4 + k, :],
                                           ident[:, :], start=True, stop=True)
                        else:
                            mm = pe.transpose(
                                wide(j % 2, P, k),
                                w2rows[:, h * 4 + k, c * EPG:(c + 1) * EPG, :].rearrange("p e h -> p (e h)"),
                                ident[:, :])
                mm.then_inc(job_done, 1)

            pe.wait_ge(ohT_ready, len(GROUPS))
            pe.wait_ge(prep_dve, PREP_OHN)
            for b in range(3):
                pe.matmul(bank(4 + b), zeros[:, 0:P], zeros[:, 0:HALF], start=True, stop=False,
                          skip_group_check=True)

            def turn(t):
                pe.wait_ge(xn1_ready, count_of(t, 1, 1))
                for h in range(2):
                    wait(pe, x1T_ready, count_of(t - 1, 2, h + 1))
                    for c in range(CH):
                        mm = pe.transpose(wide(h, P, c), xn1[t.slot][:, h * CH + c, 0:P], ident[:, :])
                    mm.then_inc(x1_turned, 1)

            def keyval(t, rows):
                pe.wait_ge(phik_ready, count_of(t, 2, 2))
                for c in range(C):
                    mm = pe.matmul(bank(4 + c // 3)[:, (c % 3) * (P + 1):(c % 3 + 1) * (P + 1)],
                                   phi1[t.slot][0:rows, c * P:(c + 1) * P], xn1[t.slot][0:rows, c, :],
                                   start=False, stop=False, skip_group_check=True)
                mm.then_inc(kv_done, 1)

            pe.wait_ge(job_lo, len(JOBS))
            pe.wait_ge(bd_loaded, 16 * 2 * BD)
            turn(Tile(0))

            def step(t):
                if (t - 2).within(NT):
                    keyval(t - 2, P)
                for h in range(2):
                    pe.wait_ge(x1T_ready, count_of(t, 2, h + 1))
                    wait(pe, phik_ready, count_of(t - 1, 2, h + 1))
                    for c in range(CH):
                        mm = pe.matmul(wide(2 + h, P, c), x1T[:, h * CH + c, :], wkbd[:, h * CH + c, :],
                                       start=True, stop=True)
                    mm.then_inc(k_done, 1)
                if (t + 1).within(NT):
                    turn(t + 1)

            def edge(i, part):
                if part == 2:
                    pe.wait_ge(e_chain, i * 11 + 10)
                    wait(pe, e_out_act, i)
                    pe.matmul(bank(7), same[:, :], xe[:, 0:HALF], start=True, stop=True).then_inc(e_summed, 1)
                if part == RING:
                    pe.wait_ge(e_out_dve, i + 1)
                    pe.matmul(bank(7), same[:, :], xe[:, HALF:D], start=True, stop=True).then_inc(e_summed, 1)

            walk1(pe, step, edge)
            keyval(Tile(NT - 2), P)
            keyval(Tile(NT - 1), REM)

            pe.wait_ge(mid_dve, MID_KVN)
            for c in range(C):
                mm = pe.transpose(wide(c // CH, P, c % CH), kvn[:, c, :], ident[:, :])
            mm.then_inc(mid_pe, 1)
            pe.wait_ge(mid_act, 2)
            for c in range(C):
                mm = pe.matmul(wide(2 + c // CH, P, c % CH), wvbd[:, c, :], kvnT[:, c, :], start=True, stop=True)
            mm.then_inc(mid_pe, 1)
            pe.wait_ge(mid_dve, MID_MAX)
            for k in range(2):
                mm = pe.matmul(bank(7)[0:1, k * P:(k + 1) * P], mx[:, k:k + 1], ident[:, :], start=True, stop=True)
            mm.then_inc(mid_pe, 1)
            pe.wait_ge(mid_dve, MID_ROW)
            pe.matmul(bank(7)[:, 0:1], ones[0:1, :], row[0:1, 0:1], start=True, stop=True).then_inc(mid_pe, 1)
            for c in range(C):
                mm = pe.matmul(wide(c // CH, P, c % CH), ones[:, :], dgm[:, c, :], start=True, stop=True)
            mm.then_inc(mid_pe, 1)
            pe.wait_ge(mid_act, 4)
            pe.wait_ge(wo_loaded, 16 * WO_LOADS)
            for j in range(2 * C):
                if j >= 4:
                    pe.wait_ge(m_lo_done, j - 3)
                if j == 3:
                    pe.wait_ge(mid_dve, MID_SCALE)
                pe.matmul(bank(4 + j % 4), kvT[:, j // 2, :], worows[:, j // 2, (j % 2) * HALF:(j % 2 + 1) * HALF],
                          start=True, stop=True).then_inc(m_done, 1)

            def turn2(t, ready, what, turned, free, free_at):
                pe.wait_ge(ready, count_of(t, 1, 1))
                for h in range(2):
                    if free is not None:
                        wait(pe, free, free_at(h))
                    for c in range(CH):
                        mm = pe.transpose(wide(h, P, c), what[:, (h * CH + c) * P:(h * CH + c + 1) * P],
                                          ident[:, :])
                    mm.then_inc(turned, 1)

            def mix(t, part):
                h, quarter = part // 4, part % 4
                if quarter == 0:
                    wait(pe, mix_read, count_of(t - 1, 2, h + 1))
                    pe.wait_ge(y_lo, count_of(t, 2, 2))
                    if t.base == 0 and h == 0:
                        pe.wait_ge(m_lo_done, 2 * C)
                if quarter == 2:
                    pe.wait_ge(a_lo, count_of(t, 2, 2))
                s = t.slot
                hi, lo, u_hi, u_lo = ((yT_hi[s], yT_lo[s], w_hi, w_lo) if quarter < 2
                                      else (aT_hi[s], aT_lo[s], m_hi, m_lo))
                cols = slice(h * HALF, (h + 1) * HALF)
                for c in range((quarter % 2) * CH, (quarter % 2 + 1) * CH):
                    pe.matmul(bank(4 + h), hi[:, c, :], u_hi[:, c, cols], start=(quarter == 0 and c == 0),
                              stop=False)
                    pe.matmul(bank(4 + h), hi[:, c, :], u_lo[:, c, cols], start=False, stop=False)
                    mm = pe.matmul(bank(4 + h), lo[:, c, :], u_hi[:, c, cols], start=False,
                                   stop=(quarter == 3 and c == C - 1))
                if quarter == 3:
                    mm.then_inc(mix_done, 1)

            def thrice(o, l_hi, l_lo, r_hi, r_lo, start, stop):
                pe.matmul(o, l_hi, r_hi, start=start, stop=False)
                pe.matmul(o, l_hi, r_lo, start=False, stop=False)
                return pe.matmul(o, l_lo, r_hi, start=False, stop=stop)

            def step(t):
                now, prep, post, last = t.within(NT), (t + 1).within(NT), (t - 1).within(NT), (t - 2).within(NT)
                n, p, o = t + 1, t - 1, t - 2
                if now:
                    mix(t, 0)
                if last:
                    pe.wait_ge(gate_chain, count_of(o, GATE_N, GATE_N))
                    wait(pe, out_ready, count_of(t - 3, 2, 2))
                    for g in range(NGRP):
                        pe.transpose(ps[:, 7, g * P:(g + 1) * P],
                                     hw[:, g * EPG:(g + 1) * EPG, :].rearrange("p e h -> p (e h)"), ident[:, :])
                    pe.matmul(ps[0:3 * HID, 7, 2 * P:3 * P], sh3[:, :].bitcast(F32), ident[:, :],
                              start=True, stop=True).then_inc(h_turned, 1)
                if prep:
                    if t.base == -1:
                        pe.wait_ge(mid_act, 6)
                    turn2(n, xn_ready, xn, x_turned, a_lo, lambda h: count_of(t, 2, h + 1))
                if now:
                    mix(t, 1)
                if last:
                    pe.wait_ge(h_hi, count_of(o, 2, 2))
                    pe.wait_ge(h_lo, count_of(o, 1, 1))
                    for h in range(2):
                        cols = slice(h * HALF, (h + 1) * HALF)
                        for g in range(NGRP):
                            thrice(bank(6 + h), hwT_hi[:, g, :], hwT_lo[:, g, :], w2_hi[:, g, cols],
                                   w2_lo[:, g, cols], g == 0, False)
                        pe.matmul(bank(6 + h), sh3T[:, :], wo3[:, cols], start=False, stop=True)\
                          .then_inc(ffn_done, 1)
                if prep:
                    if t.base == -1:
                        pe.wait_ge(wq_split, 2)
                    for h in range(2):
                        pe.wait_ge(x_lo, count_of(n, 2, h + 1))
                        wait(pe, elu_ready, count_of(t, 2, h + 1))
                        for c in range(CH):
                            cc = h * CH + c
                            mm = thrice(wide(2 + h, P, c), xT_hi[:, cc, :], xT_lo[:, cc, :], wq_hi[:, cc, :],
                                        wq_lo[:, cc, :], True, True)
                        mm.then_inc(q_done, 1)
                if now:
                    mix(t, 2)
                if post:
                    free = (x_lo, lambda h: count_of(n, 2, h + 1)) if prep else (a_lo, lambda h: 2 * NT)
                    turn2(p, xn2_ready, xn2, n_turned, *free)
                if now:
                    mix(t, 3)
                if post:
                    pe.wait_ge(n_lo, count_of(p, 2, 2))
                    wait(pe, out_ready, count_of(t - 2, 2, 1))
                    for c in range(C):
                        mm = thrice(bank(6)[:, 0:FIN], nT_hi[:, c, :], nT_lo[:, c, :], fin_hi[:, c, :],
                                    fin_lo[:, c, :], c == 0, c == C - 1)
                    mm.then_inc(fin_done, 1)
                if prep:
                    free = ((n_lo, lambda h: count_of(p, 2, h + 1)) if post
                            else (x_lo, lambda h: count_of(n, 2, h + 1)))
                    turn2(n, y_ready, gin[n.slot], y_turned, *free)
                if now:
                    mix(t, 4)
                    mix(t, 5)
                if now:
                    mix(t, 6)
                if prep:
                    turn2(n, a_ready, phi, a_turned, y_lo, lambda h: count_of(n, 2, h + 1))
                if now:
                    mix(t, 7)

            walk2(pe, step)

        @block.vector
        def _(dve):
            def chain(s, start=0):
                state = [start]

                def do(inst):
                    inst.then_inc(s, 1)
                    state[0] = state[0] + 1
                    dve.wait_ge(s, state[0])
                return do, state

            dve.memset(zeros, 0.0).then_inc(consts_dve, 1)
            dve.memset(bdmask[:, :], 0.0).then_inc(consts_dve, 1)
            dve.memset(ones[:, :], 1.0).then_inc(consts_dve, 1)
            dve.wait_ge(consts_dve, 2)
            for k in range(2):
                dve.memset(bdmask[k * DH:(k + 1) * DH, k * DH:(k + 1) * DH], 1.0).then_inc(consts_dve, 1)
            dve.memset(pen_a[:, 0:EPG], -BIG).then_inc(consts_dve, 1)
            dve.memset(pen_a[:, EPG:], BIG).then_inc(consts_dve, 1)
            dve.memset(pen_b[:, 0:EPG], 0.0).then_inc(consts_dve, 1)
            dve.memset(pen_b[:, EPG:], -BIG).then_inc(consts_dve, 1)
            dve.memset(row[:, :], 0.0).then_inc(consts_dve, 1)
            dve.memset(mx[:, :], 0.0).then_inc(consts_dve, 1)
            dve.memset(dve_cell[:, :], 0.0).then_inc(consts_dve, 1)

            do, at = chain(prep_dve)
            dve.wait_ge(consts_dve, 12)
            dve.wait_ge(prep_pool, 6)
            dve.wait_ge(idx_loaded, 32)
            do(dve.tensor_copy(src_f[:, :], src_i[:, :]))
            do(dve.tensor_scalar(ab_i[:, 0, :], src_i[:, :], 7, None, ALU.logical_shift_right))
            do(dve.tensor_scalar(ab_i[:, 1, :], src_i[:, :], P - 1, None, ALU.bitwise_and))
            do(dve.tensor_copy(ab_f[:, :, :], ab_i[:, :, :]))
            do(dve.tensor_copy(iota_f[:, :], iota_i[:, :]))
            do(dve.tensor_copy(dump_f[:, :], dump_i[:, :]))
            do(dve.tensor_tensor(oha, iota_f[:, None, 0:NT].to_broadcast([P, ET, NT]),
                                 ab_f[:, 0, :, None].to_broadcast([P, ET, NT]), ALU.is_equal))
            do(dve.tensor_tensor(ohb, iota_f[:, None, :].to_broadcast([P, ET, P]),
                                 ab_f[:, 1, :, None].to_broadcast([P, ET, P]), ALU.is_equal))
            assert at[0] == PREP_HOT
            do(dve.tensor_scalar(ab_i[:, 0, :], dst_i[:, :], 7, None, ALU.logical_shift_right))
            do(dve.tensor_scalar(ab_i[:, 1, :], dst_i[:, :], P - 1, None, ALU.bitwise_and))
            do(dve.tensor_copy(ab_f[:, :, :], ab_i[:, :, :]))
            do(dve.tensor_tensor(oha_dst, iota_f[:, None, 0:NT].to_broadcast([P, ET, NT]),
                                 ab_f[:, 0, :, None].to_broadcast([P, ET, NT]), ALU.is_equal))
            do(dve.tensor_tensor(ohb_dst, iota_f[:, None, :].to_broadcast([P, ET, P]),
                                 ab_f[:, 1, :, None].to_broadcast([P, ET, P]), ALU.is_equal))
            assert at[0] == PREP_HOT_DST
            dve.wait_ge(prep_pe, 1)
            do(dve.tensor_scalar(dis[:, :], bank(2)[:, 0:NT], 1.0, None, ALU.add))
            assert at[0] == PREP_DEG

            def max_abs(o, i):
                return dve.tensor_reduce(o, i, AX_X, ALU.max, apply_absolute_value=True)

            def power_of_two(do, v, factor, top):
                do(dve.tensor_scalar(v, v, factor, 1e-25, ALU.mult, ALU.max))
                do(dve.reciprocal(v, v))
                do(dve.tensor_scalar(v, v, top, None, ALU.mult))
                do(dve.tensor_scalar(v.bitcast(I32), v.bitcast(I32), 0x7F800000, None, ALU.bitwise_and))

            dve.wait_ge(wq_loaded, 16 * BD)
            do(max_abs(mx[:, 1:2], wqbd.rearrange("p c n -> p (c n)")))
            dve.wait_ge(cat_loaded, 16 * 4)
            do(max_abs(mx[:, 2:3], wcat1[:, :]))
            do(max_abs(mx[0:NGRP + NEXP, 3:4], wcat2))
            dve.wait_ge(w_loaded, 16)
            do(max_abs(mx[:, 0:1], wrows.rearrange("p o i -> p (o i)")))
            assert at[0] == PREP_MAX
            dve.wait_ge(prep_pe, 3)
            do(dve.tensor_reduce(row[0:1, 0:NMAX], bank(3)[0:1, 0:NMAX * P].rearrange("p (k n) -> p k n", k=NMAX),
                                 AX_X, ALU.max))
            do(dve.tensor_tensor(row[0:1, 2:3], row[0:1, 2:3], row[0:1, 3:4], ALU.max))
            power_of_two(do, row[0:1, 0:3], 1.0, W_TOP)
            assert at[0] == PREP_POW
            dve.wait_ge(prep_pe, 4)
            do(dve.tensor_copy(sc[:, 0:3], bank(3)[:, 0:3]))
            assert at[0] == PREP_SCALE
            do(dve.reciprocal(sc[:, 8:10], sc[:, 1:3]))
            do(dve.tensor_scalar(sc[:, 8:10], sc[:, 8:10], 1.0 / LN_SCALE, None, ALU.mult))
            do(dve.tensor_scalar(sc[:, 10:12], sc[:, 8:10], -1.0, None, ALU.mult))

            dve.wait_ge(prep_pe, 2)
            do(dve.tensor_copy(disT[:, :], bank(2)[0:NT, 0:P]))
            assert at[0] == PREP_DIST

            def statistics(t):
                dve.wait_ge(x1_loaded[t.slot], t.turn * 16 + 16)
                wait(dve, mv_kept, count_of(t - RING, 1, 1))
                wait(dve, xn1_ready, count_of(t - RING, 1, 1))
                for h in range(2):
                    o = dve.bn_stats(stats[:, h, :], xin[t.slot][:, h * HALF:(h + 1) * HALF])
                m = mv[t.slot]
                o.then_inc(stats1_done, 1)
                dve.wait_ge(stats1_done, count_of(t, 2, 1))
                carry(dve, dve_cell)
                dve.bn_aggr(m[:, :], stats[:, :, :]).then_inc(stats1_done, 1)
                dve.wait_ge(stats1_done, count_of(t, 2, 2))
                dve.tensor_scalar(m[:, 1:2], m[:, 1:2], LN_EPS, None, ALU.add).then_inc(var1_ready, 1)
                dve.tensor_scalar(m[:, 0:1], m[:, 0:1], -1.0, None, ALU.mult).then_inc(var1_ready, 1)

            for j, (kind, c, h) in enumerate(JOBS):
                dve.wait_ge(job_hi, j + 1)
                b = bank(j % 2)
                cols = slice(h * HALF, (h + 1) * HALF)
                if kind == "w":
                    o = dve.scalar_tensor_tensor(w_lo[:, c, cols], b, s_w, w_hi[:, c, cols], ALU.mult, ALU.subtract)
                elif kind == "fin":
                    o = dve.scalar_tensor_tensor(fin_lo[:, c, :], b[:, 0:FIN], s_f, fin_hi[:, c, :], ALU.mult,
                                                 ALU.subtract)
                elif kind == "wo":
                    third = wo3[2 * HID:3 * HID, cols]
                    o = dve.tensor_tensor(third, b[2 * HID:3 * HID, :], third.bitcast(F32), ALU.subtract)
                else:
                    o = dve.tensor_tensor(w2_lo[:, c, cols], b, w2_hi[:, c, cols].bitcast(F32), ALU.subtract)
                o.then_inc(job_lo, 1)
                if j < len(GROUPS):
                    end, k0, k1 = GROUPS[j]
                    hot, got = (ohb, dis_src) if end == "src" else (ohb_dst, dis_dst)
                    dve.wait_ge(dis_picked, j + 1)
                    do(dve.tensor_tensor(ohb_dst[:, k0:k1, :],
                                         bank(6 + j % 2)[:, 0:(k1 - k0) * P].rearrange("p (t b) -> p t b", b=P),
                                         hot[:, k0:k1, :], ALU.mult))
                    do(dve.tensor_reduce(got[:, k0:k1], ohb_dst[:, k0:k1, :], AX_X, ALU.add))
                if j == len(GROUPS):
                    do(dve.tensor_tensor(norm[:, :], dis_src[:, :], dis_dst[:, :], ALU.mult))
                    do(dve.tensor_tensor(dis2[:, :], dis[:, :], dis[:, :], ALU.mult))
                    do(dve.tensor_tensor(ohn, oha, norm[:, :, None].to_broadcast([P, ET, NT]), ALU.mult))
                    assert at[0] == PREP_OHN
            statistics(Tile(0))
            dve.wait_ge(prep_pe, 5)
            do(dve.tensor_tensor(rowsum[:, :], bank(3)[:, 0:NT], dis2[:, :], ALU.add))
            for s in range(RING):
                do(dve.memset(xn1[s][:, :, P:P + 1], 1.0))
            assert at[0] == PREP_ALL

            statistics(Tile(1))
            dve.tensor_scalar(wq_hi[:, :, :], wqbd, s_q, None, ALU.mult).then_inc(wq_split, 1)
            dve.wait_ge(wq_split, 1)
            dve.scalar_tensor_tensor(wq_lo[:, :, :], wqbd, s_q, wq_hi[:, :, :], ALU.mult, ALU.subtract)\
               .then_inc(wq_split, 1)

            def phi_k(t):
                for h in range(2):
                    cols = slice(h * HALF, (h + 1) * HALF)
                    dve.wait_ge(kexp_done, count_of(t, 2, h + 1))
                    dve.scalar_tensor_tensor(phi1[t.slot][:, cols], bank(2 + h), 0.0, ex1[:, cols], ALU.max, ALU.add)\
                       .then_inc(phik_ready, 1)

            def step(t):
                if (t - 1).within(NT):
                    phi_k(t - 1)
                if (t + 2).within(NT):
                    statistics(t + 2)
                if t.i is None and t.base >= P1_LAST + WO_LOADS:
                    dve.wait_ge(wo_loaded, 16 * WO_LOADS)
                    k, n = t.base - P1_LAST - WO_LOADS, NT - P1_LAST - WO_LOADS
                    for c in range(k * C // n, (k + 1) * C // n):
                        do_mid(max_abs(mxo[:, c:c + 1], worows[:, c, :]))

            def edge(i, part):
                def col(k):
                    return e_sc[:, k:k + 1]

                src_c, norm_c, dup_c, gap_c, rn_c = [col(k) for k in range(5)]
                one = bass.ds(i, 1)
                if part == 0:
                    dve.tensor_copy(e_dst[:, :], dst_i[:, one]).then_inc(e_cols, 1)
                    dve.tensor_copy(src_c, src_f[:, one]).then_inc(e_cols, 1)
                    dve.tensor_copy(norm_c, norm[:, one]).then_inc(e_cols, 1)
                if part == 1:
                    dve.wait_ge(e_cols, i * 3 + 3)
                    wait(dve, e_summed, i * 2)
                    do, _ = chain(e_chain, i * 11)
                    do(dve.tensor_scalar(same[:, :], srcb[:, :, one].rearrange("p e o -> p (e o)"), src_c, None,
                                         ALU.is_equal))
                    do(dve.tensor_tensor(same_t[:, :], same[:, :], below[:, :], ALU.mult))
                    do(dve.tensor_reduce(dup_c, same_t[:, :], AX_X, ALU.add))
                    do(dve.tensor_scalar(dup_c, dup_c, 1.0, None, ALU.min))
                    do(dve.tensor_scalar(gap_c, dump_f[:, :], src_c, None, ALU.subtract))
                    dve.wait_ge(e_gathered, i * 16 + 16)
                    dve.bn_stats(e_stats[:, 0, :], xe[:, 0:HALF])
                    do(dve.bn_stats(e_stats[:, 1, :], xe[:, HALF:D]))
                    carry(dve, dve_cell)
                    do(dve.bn_aggr(e_mv[:, :], e_stats[:, :, :]))
                    do(dve.tensor_scalar(e_mv[:, 1:2], e_mv[:, 1:2], LN_EPS, None, ALU.add))
                if part == 2:
                    dve.wait_ge(e_rstd, i + 1)
                    do, _ = chain(e_chain, i * 11 + 8)
                    do(dve.tensor_tensor(rn_c, e_mv[:, 1:2], norm_c, ALU.mult))
                    do(dve.tensor_scalar(xe[:, :], xe[:, :], e_mv[:, 0:1], rn_c, ALU.subtract, ALU.mult))
                    wait(dve, agg_added, i * 16)
                    do(dve.tensor_scalar(e_idx[:, :], dup_c, gap_c, src_c, ALU.mult, ALU.add))
                if part == RING:
                    dve.wait_ge(e_summed, i * 2 + 1)
                    dve.tensor_copy(msum[:, 0:HALF], bank(7)).then_inc(e_out_dve, 1)

            dve.wait_ge(srcb_loaded, 16)
            do_mid, at_mid = chain(mid_dve)
            edge(0, 0)
            walk1(dve, step, edge)
            phi_k(Tile(NT - 1))

            do, at = do_mid, at_mid
            dve.wait_ge(kv_done, NT)
            for b in range(3):
                do(dve.tensor_copy(ks[:, 3 * b:3 * b + (3 if b < 2 else 2)],
                                   bank(4 + b)[:, P:(3 if b < 2 else 2) * (P + 1):P + 1]))
            do(dve.tensor_scalar(rk[:, 0:C], ks[:, 0:C], 1e-37, None, ALU.max))
            do(dve.reciprocal(rk[:, 0:C], rk[:, 0:C]))
            for c in range(C):
                do(dve.scalar_tensor_tensor(kvn[:, c, :], bank(4 + c // 3)[:, (c % 3) * (P + 1):(c % 3) * (P + 1) + P],
                                            rk[:, c:c + 1], bdmask[:, :], ALU.mult, ALU.mult))
            assert at[0] == MID_KVN
            for c in range(C):
                do(dve.tensor_scalar(dgm[:, c, :], ident[:, :], ks[:, c:c + 1], None, ALU.mult))
            dve.wait_ge(mid_act, 4)
            do(max_abs(mx[:, 0:1], phi[:, :]))
            do(dve.tensor_reduce(mx[:, 1:2], mxo[:, :], AX_X, ALU.max))
            assert at[0] == MID_MAX
            dve.wait_ge(mid_pe, 3)
            for k in range(2):
                do(dve.tensor_reduce(row[0:1, k:k + 1], bank(7)[0:1, k * P:(k + 1) * P], AX_X, ALU.max))
            do(dve.tensor_tensor(row[0:1, 0:1], row[0:1, 0:1], row[0:1, 1:2], ALU.mult))
            power_of_two(do, row[0:1, 0:1], float(DH), W_TOP)
            assert at[0] == MID_ROW
            dve.wait_ge(mid_pe, 4)
            do(dve.tensor_copy(s_m, bank(7)[:, 0:1]))
            assert at[0] == MID_SCALE
            do(dve.tensor_scalar(tmp0, s_w, Y_SCALE_MAX, None, ALU.mult))
            do(dve.tensor_scalar(tmp1, s_m, A_SCALE_MAX, None, ALU.mult))
            do(dve.tensor_tensor(s_t, tmp0, tmp1, ALU.min))
            do(dve.reciprocal(t_inv, s_t))
            do(dve.reciprocal(tmp0, s_w))
            do(dve.tensor_tensor(s_y, s_t, tmp0, ALU.mult))
            do(dve.reciprocal(tmp1, s_m))
            do(dve.tensor_tensor(s_a, s_t, tmp1, ALU.mult))
            assert at[0] == MID_ALL
            for j in range(2 * C):
                dve.wait_ge(m_hi_done, j + 1)
                cols = slice((j % 2) * HALF, (j % 2 + 1) * HALF)
                dve.scalar_tensor_tensor(m_lo[:, j // 2, cols], bank(4 + j % 4), s_m, m_hi[:, j // 2, cols],
                                         ALU.mult, ALU.subtract).then_inc(m_lo_done, 1)

            dve.wait_ge(bias_loaded, 16)

            def low(t, hi_done, done, hi, lo, scale):
                for h in range(2):
                    dve.wait_ge(hi_done, count_of(t, 2, h + 1))
                    o = lo[:, h * CH:(h + 1) * CH, :].rearrange("p c n -> p (c n)")
                    g = hi[:, h * CH:(h + 1) * CH, :].rearrange("p c n -> p (c n)")
                    dve.scalar_tensor_tensor(o, bank(h), scale, g, ALU.mult, ALU.subtract).then_inc(done, 1)

            def mixed(t, h):
                cols = slice(h * HALF, (h + 1) * HALF)
                x_ = xp[t.slot][:, cols]
                dve.wait_ge(mix_done, count_of(t, 2, h + 1))
                if t.i is not None or t.turn >= 1:
                    dve.wait_ge(stored[t.slot], t.turn * 16)
                dve.scalar_tensor_tensor(x_, bank(4 + h), t_inv, xin[t.slot][:, cols], ALU.mult, ALU.add)\
                   .then_inc(mix_read, 1)
                dve.wait_ge(mix_read, count_of(t, 2, h + 1))
                dve.scalar_tensor_tensor(x_, bias_b[:, cols], rowsum[:, bass.ds(t.n, 1)], x_, ALU.mult, ALU.add)\
                   .then_inc(xp_ready, 1)
                dve.wait_ge(xp_ready, count_of(t, 2, h + 1))
                return dve.bn_stats(stats2[:, h, :], x_)

            def gate_in(p):
                do, at = chain(gate_chain, count_of(p, GATE_N, 0))
                f = bank(6)
                dve.wait_ge(fin_done, count_of(p, 1, 1))
                do(dve.scalar_tensor_tensor(lg[:, :], f[:, 4 * HID:FIN], f_inv, gbias[:, :], ALU.mult, ALU.add))
                do(dve.tensor_scalar(gs[:, 0:1], lg[:, 1:2], lg[:, 0:1], None, ALU.subtract))
                do(dve.tensor_scalar(gs[:, 1:2], gs[:, 0:1], 0.0, None, ALU.is_gt))
                do(dve.scalar_tensor_tensor(exb[:, 0:1], gs[:, 0:1], -1.0, gs[:, 0:1], ALU.mult, ALU.min))
                do(dve.scalar_tensor_tensor(v8[:, :], pen_a[:, :], gs[:, 1:2], pen_b[:, :], ALU.mult, ALU.add))
                do(dve.tensor_tensor(v8[:, :], v8[:, :], lg[:, NGRP:], ALU.add))
                do(dve.tensor_reduce(gs[:, 2:3], v8[:, :], AX_X, ALU.max))
                do(dve.tensor_scalar(exb[:, 1 + NSIL:], v8[:, :], gs[:, 2:3], None, ALU.subtract))
                do(dve.tensor_scalar(exb[:, 1:1 + NSIL].rearrange("p (k h) -> p k h", k=2),
                                     f[:, 0:4 * HID].rearrange("p (k h) -> p k h", k=2)[:, :, 0:HID],
                                     f_ninv, 80.0, ALU.mult, ALU.min))

            def gate_out(p):
                do, at = chain(gate_chain, count_of(p, GATE_N, GATE_EXP))
                ab = bank(6)[:, 0:4 * HID].rearrange("p (k h) -> p k h", k=2)
                hs2 = hs[:, :].rearrange("p (k h) -> p k h", k=2)
                pe8 = exb[:, 1 + NSIL:]
                dve.wait_ge(gate_exp, count_of(p, 1, 1))
                do(dve.tensor_scalar(rec[:, :], exb[:, 0:1 + NSIL], 1.0, None, ALU.add))
                do(dve.reciprocal(rec[:, :], rec[:, :]))
                do(dve.scalar_tensor_tensor(hs2, ab[:, :, 0:HID], f_inv,
                                            rec[:, 1:].rearrange("p (k h) -> p k h", k=2), ALU.mult, ALU.mult))
                do(dve.scalar_tensor_tensor(hs2, ab[:, :, HID:2 * HID], f_inv, hs2, ALU.mult, ALU.mult))
                other = pe8[:, None, :].to_broadcast([P, NEXP, NEXP])
                mine = pe8[:, :, None].to_broadcast([P, NEXP, NEXP])
                do(dve.tensor_tensor(gt[:, :, :], other, mine, ALU.is_gt))
                do(dve.tensor_tensor(eq[:, :, :], other, mine, ALU.is_equal))
                do(dve.tensor_tensor(eq[:, :, :], eq[:, :, :], tri[:, :, :], ALU.mult))
                do(dve.tensor_tensor(gt[:, :, :], gt[:, :, :], eq[:, :, :], ALU.add))
                do(dve.tensor_reduce(rank[:, :], gt[:, :, :], AX_X, ALU.add))
                do(dve.scalar_tensor_tensor(rank[:, :], rank[:, :], 2.0, pe8, ALU.is_lt, ALU.mult))
                do(dve.tensor_reduce(gs[:, 3:4], pe8, AX_X, ALU.add))
                do(dve.reciprocal(gs[:, 4:5], gs[:, 3:4]))
                do(dve.tensor_tensor(gs[:, 5:6], gs[:, 4:5], rec[:, 0:1], ALU.mult))
                do(dve.tensor_scalar(rank[:, :], rank[:, :], gs[:, 5:6], None, ALU.mult))
                wait(dve, h_turned, count_of(p - 1, 1, 1))
                do(dve.tensor_tensor(hw[:, :, :], hs[:, None, HID:].to_broadcast([P, NEXP, HID]),
                                     rank[:, :, None].to_broadcast([P, NEXP, HID]), ALU.mult))
                do(dve.tensor_copy(sh3[:, 0:HID], hs[:, 0:HID]))
                do(dve.tensor_tensor(sh3[:, HID:2 * HID], hs[:, 0:HID], sh3[:, 0:HID].bitcast(F32), ALU.subtract))
                do(dve.tensor_copy(sh3[:, 2 * HID:], hs[:, 0:HID]))

            def step(t):
                now, prep, post, last = t.within(NT), (t + 1).within(NT), (t - 1).within(NT), (t - 2).within(NT)
                n, p, o = t + 1, t - 1, t - 2
                if post:
                    mixed(p, 1).then_inc(ln2_chain, 1)
                    dve.wait_ge(ln2_chain, count_of(p, 3, 1))
                    carry(dve, dve_cell)
                    dve.bn_aggr(mv2[:, :], stats2[:, :, :]).then_inc(ln2_chain, 1)
                    dve.wait_ge(ln2_chain, count_of(p, 3, 2))
                    dve.tensor_scalar(mv2[:, 1:2], mv2[:, 1:2], LN_EPS, None, ALU.add).then_inc(ln2_chain, 1)
                if last:
                    dve.wait_ge(h_hi, count_of(o, 2, 2))
                    dve.tensor_tensor(hwT_lo[:, :, :].rearrange("p c n -> p (c n)"), ps[:, 7, 0:2 * P],
                                      hwT_hi[:, :, :].rearrange("p c n -> p (c n)").bitcast(F32), ALU.subtract)\
                       .then_inc(h_lo, 1)
                if prep:
                    low(n, x_hi, x_lo, xT_hi, xT_lo, LN_SCALE)
                if post:
                    dve.wait_ge(rstd2_ready, count_of(p, 1, 1))
                    wait(dve, n_turned, count_of(t - 2, 2, 2))
                    dve.tensor_scalar(xn2[:, :], xp[p.slot][:, :], mv2[:, 0:1], mv2[:, 1:2], ALU.subtract,
                                      ALU.mult).then_inc(xn2_ready, 1)
                if prep:
                    dve.wait_ge(g_loaded[n.slot], n.turn * 16 + 16)
                    dve.scalar_tensor_tensor(gin[n.slot], xn[:, :], dis2[:, bass.ds(n.n, 1)], gin[n.slot],
                                             ALU.mult, ALU.add).then_inc(y_ready, 1)
                if last:
                    for h in range(2):
                        x_ = xp[o.slot][:, h * HALF:(h + 1) * HALF]
                        dve.wait_ge(ffn_done, count_of(o, 2, h + 1))
                        dve.tensor_tensor(x_, bank(6 + h), x_, ALU.add).then_inc(out_ready, 1)
                if prep:
                    for h in range(2):
                        cols = slice(h * HALF, (h + 1) * HALF)
                        dve.wait_ge(qexp_done, count_of(n, 2, h + 1))
                        dve.scalar_tensor_tensor(phi[:, cols], bank(2 + h), q_inv, phi[:, cols], ALU.mult, ALU.max)\
                           .then_inc(elu_ready, 1)
                if post:
                    low(p, n_hi, n_lo, nT_hi, nT_lo, LN_SCALE)
                if prep:
                    if t.base == -1:
                        dve.wait_ge(mid_act, 6)
                    dve.wait_ge(elu_ready, count_of(n, 2, 2))
                    dve.scalar_tensor_tensor(phi[:, :], phi[:, :], 1.0, ksb[:, :], ALU.add, ALU.mult)\
                       .then_inc(z_chain, 1)
                    dve.wait_ge(z_chain, count_of(n, 4, 1))
                    dve.tensor_reduce(z16[:, :], phi[:, :].rearrange("p (h d) -> p h d", d=DH), AX_X, ALU.add)\
                       .then_inc(z_chain, 1)
                    dve.wait_ge(z_chain, count_of(n, 4, 2))
                    dve.tensor_scalar(z16[:, :], z16[:, :], Z_EPS, None, ALU.add).then_inc(z_chain, 1)
                    dve.wait_ge(z_chain, count_of(n, 4, 3))
                    dve.reciprocal(z16[:, :], z16[:, :]).then_inc(z_chain, 1)
                if now:
                    mixed(t, 0)
                if prep:
                    low(n, y_hi, y_lo, yT_hi[n.slot], yT_lo[n.slot], s_y)
                if post:
                    gate_in(p)
                    gate_out(p)
                if prep:
                    low(n, a_hi, a_lo, aT_hi[n.slot], aT_lo[n.slot], s_a)

            walk2(dve, step)


_INS = ['x', 'src', 'dst', 'L0_gnn_W', 'L0_gnn_b', 'L0_mix_Wq', 'L0_mix_Wk', 'L0_mix_Wv', 'L0_mix_Wo',
        'L0_ffn_w_in', 'L0_ffn_w_out', 'L0_ffn_w1', 'L0_ffn_w2', 'L0_ffn_wg', 'L0_ffn_we', 'L0_ffn_gb', 'L0_ffn_eb']


def kernel(**inputs):
    import numpy as _np
    import concourse.bacc as _bacc
    from concourse import mybir as _mybir
    from concourse.bass_utils import run_bass_kernel_spmd as _run

    nc = _bacc.Bacc("TRN2", target_bir_lowering=False, num_devices=1)
    arrays, args = {}, []
    for name in _INS:
        a = _np.ascontiguousarray(inputs[name])
        arrays[f"in_{name}_dram"] = a
        args.append(nc.dram_tensor(f"in_{name}_dram", a.shape, _mybir.dt.from_np(a.dtype), kind="ExternalInput").ap())
    shape = inputs["x"].shape
    args.append(nc.dram_tensor("out_0_dram", shape, _mybir.dt.float32, kind="ExternalOutput").ap())
    gps_layer(nc, *args)
    r = _run(nc, [arrays], core_ids=[0])
    return r.results[0]["out_0_dram"]
```
